# Optimizing a Trainium2 kernel written in Bass

```python
import numpy as np
import jax
import jax.numpy as jnp

def _softmax(x, axis=-1):
    return jax.nn.softmax(x, axis=axis)

def _gelu(x):
    return jax.nn.gelu(x, approximate=True)

def _silu(x):
    return jax.nn.silu(x)

def _sigmoid(x):
    return jax.nn.sigmoid(x)

def _layernorm(x, axis=-1, eps=1e-05):
    m = jnp.mean(x, axis=axis, keepdims=True)
    v = jnp.var(x, axis=axis, keepdims=True)
    return (x - m) / jnp.sqrt(v + eps)

def _scatter_add(tgt, idx, src, axis=0):
    return tgt.at[idx].add(src)

def _segment_sum(src, seg, n):
    return jax.ops.segment_sum(src, seg, n)
kernel_name = 'mk_macaron_d1_jaxref_r8_1e8380'

def setup_inputs(seed: int=0):
    np.random.seed(seed)
    _w = jnp.asarray

    def _L0_attn_setup():
        import jax, jax.numpy as jnp
        import numpy as np
        D_MODEL, D_STATE, D_CONV, EXPAND = (128, 16, 4, 2)
        D_INNER = EXPAND * D_MODEL
        DT_RANK = (D_MODEL + 15) // 16
        B, L = (2, 256)

        def _mamba(x, in_w, conv_w, conv_b, xp_w, dtp_w, dtp_b, A_log, Dp, out_w):
            di = A_log.shape[0]
            n = A_log.shape[1]
            r = dtp_w.shape[1]
            xz = x @ in_w.T
            xi, z = jnp.split(xz, 2, axis=-1)
            xc = jnp.transpose(xi, (0, 2, 1))
            xc = jax.lax.conv_general_dilated(xc, conv_w, window_strides=(1,), padding=[(conv_w.shape[-1] - 1, 0)], dimension_numbers=('NCH', 'OIH', 'NCH'), feature_group_count=di)
            xc = jax.nn.silu(xc + conv_b[None, :, None])
            xc = jnp.transpose(xc, (0, 2, 1))
            x_dbl = xc @ xp_w.T
            dt = x_dbl[..., :r]
            Bm = x_dbl[..., r:r + n]
            Cm = x_dbl[..., r + n:]
            delta = jax.nn.softplus(dt @ dtp_w.T + dtp_b)
            A = -jnp.exp(A_log)

            def step(h, inp):
                u_t, d_t, b_t, c_t = inp
                dA = jnp.exp(d_t[:, :, None] * A)
                h = h * dA + (d_t * u_t)[:, :, None] * b_t[:, None, :]
                y = jnp.einsum('bdn,bn->bd', h, c_t)
                return (h, y)
            h0 = jnp.zeros((x.shape[0], di, n), x.dtype)
            ins = (jnp.transpose(xc, (1, 0, 2)), jnp.transpose(delta, (1, 0, 2)), jnp.transpose(Bm, (1, 0, 2)), jnp.transpose(Cm, (1, 0, 2)))
            _, ys = jax.lax.scan(step, h0, ins)
            y = jnp.transpose(ys, (1, 0, 2)) + xc * Dp
            y = y * jax.nn.silu(z)
            return y @ out_w.T

        def _mamba_params(key):
            ks = jax.random.split(key, 7)
            s = 0.02
            in_w = jax.random.normal(ks[0], (2 * D_INNER, D_MODEL), jnp.float32) * s
            conv_w = jax.random.normal(ks[1], (D_INNER, 1, D_CONV), jnp.float32) * 0.2
            conv_b = jnp.zeros((D_INNER,), jnp.float32)
            xp_w = jax.random.normal(ks[2], (DT_RANK + 2 * D_STATE, D_INNER), jnp.float32) * s
            dtp_w = jax.random.normal(ks[3], (D_INNER, DT_RANK), jnp.float32) * 0.1
            dtp_b = jax.random.normal(ks[4], (D_INNER,), jnp.float32) * 0.1 - 4.0
            A_log = jnp.broadcast_to(jnp.log(jnp.arange(1, D_STATE + 1, dtype=jnp.float32)), (D_INNER, D_STATE)).copy()
            Dp = jnp.ones((D_INNER,), jnp.float32)
            out_w = jax.random.normal(ks[5], (D_MODEL, D_INNER), jnp.float32) * s
            return (in_w, conv_w, conv_b, xp_w, dtp_w, dtp_b, A_log, Dp, out_w)
        key = jax.random.key(seed)
        kx, k1, k2 = jax.random.split(key, 3)
        x = jax.random.normal(kx, (B, L, D_MODEL), jnp.float32)
        p1 = _mamba_params(k1)
        p2 = _mamba_params(k2)
        names = ['in_w', 'conv_w', 'conv_b', 'xp_w', 'dtp_w', 'dtp_b', 'A_log', 'Dvec', 'out_w']
        d = {'x': x}
        for n, v in zip([s + '1' for s in names], p1):
            d[n] = v
        for n, v in zip([s + '2' for s in names], p2):
            d[n] = v
        return d
    _L0_attn_in = _L0_attn_setup()

    def _L0_ffn_setup():
        import jax, jax.numpy as jnp
        import numpy as np
        B, S, H = (2, 256, 128)
        E, I, K = (8, 512, 2)

        def _moe_forward(x, gate_w, wg, wu, wd):
            b, s, h = x.shape
            x_flat = x.reshape(-1, h)
            logits = x_flat @ gate_w.T
            top_v, top_i = jax.lax.top_k(logits, K)
            probs = jax.nn.softmax(top_v.astype(jnp.float32), axis=-1).astype(logits.dtype)
            one_hot = jax.nn.one_hot(top_i, E, dtype=probs.dtype)
            combine = jnp.einsum('tk,tke->et', probs, one_hot)

            def body(acc, ws):
                wge, wue, wde, we = ws
                hidden = jax.nn.silu(x_flat @ wge.T) * (x_flat @ wue.T)
                return (acc + we[:, None] * (hidden @ wde.T), None)
            out, _ = jax.lax.scan(body, jnp.zeros_like(x_flat), (wg, wu, wd, combine))
            return out.reshape(b, s, h)
        key = jax.random.key(seed)
        ks = jax.random.split(key, 5)
        scale_h = 1.0 / np.sqrt(H)
        scale_i = 1.0 / np.sqrt(I)
        x = jax.random.normal(ks[0], (B, S, H), dtype=jnp.float32)
        gate_w = jax.random.normal(ks[1], (E, H), dtype=jnp.float32) * scale_h
        wg = jax.random.normal(ks[2], (E, I, H), dtype=jnp.float32) * scale_h
        wu = jax.random.normal(ks[3], (E, I, H), dtype=jnp.float32) * scale_h
        wd = jax.random.normal(ks[4], (E, H, I), dtype=jnp.float32) * scale_i
        return {'x': x, 'gate_w': gate_w, 'wg': wg, 'wu': wu, 'wd': wd}
    _L0_ffn_in = _L0_ffn_setup()
    _d = {'L0_attn_x': _L0_attn_in['x'], 'L0_attn_in_w1': _L0_attn_in['in_w1'], 'L0_attn_conv_w1': _L0_attn_in['conv_w1'], 'L0_attn_conv_b1': _L0_attn_in['conv_b1'], 'L0_attn_xp_w1': _L0_attn_in['xp_w1'], 'L0_attn_dtp_w1': _L0_attn_in['dtp_w1'], 'L0_attn_dtp_b1': _L0_attn_in['dtp_b1'], 'L0_attn_A_log1': _L0_attn_in['A_log1'], 'L0_attn_Dvec1': _L0_attn_in['Dvec1'], 'L0_attn_out_w1': _L0_attn_in['out_w1'], 'L0_attn_in_w2': _L0_attn_in['in_w2'], 'L0_attn_conv_w2': _L0_attn_in['conv_w2'], 'L0_attn_conv_b2': _L0_attn_in['conv_b2'], 'L0_attn_xp_w2': _L0_attn_in['xp_w2'], 'L0_attn_dtp_w2': _L0_attn_in['dtp_w2'], 'L0_attn_dtp_b2': _L0_attn_in['dtp_b2'], 'L0_attn_A_log2': _L0_attn_in['A_log2'], 'L0_attn_Dvec2': _L0_attn_in['Dvec2'], 'L0_attn_out_w2': _L0_attn_in['out_w2'], 'L0_ffn_gate_w': _L0_ffn_in['gate_w'], 'L0_ffn_wg': _L0_ffn_in['wg'], 'L0_ffn_wu': _L0_ffn_in['wu'], 'L0_ffn_wd': _L0_ffn_in['wd']}
    _x0 = _d['L0_attn_x']
    _d['L0_attn_x'] = jax.random.normal(jax.random.fold_in(jax.random.key(seed), 1), (32, 256, 128), dtype=_x0.dtype)
    del _x0
    return _d

def reference(L0_attn_x, L0_attn_in_w1, L0_attn_conv_w1, L0_attn_conv_b1, L0_attn_xp_w1, L0_attn_dtp_w1, L0_attn_dtp_b1, L0_attn_A_log1, L0_attn_Dvec1, L0_attn_out_w1, L0_attn_in_w2, L0_attn_conv_w2, L0_attn_conv_b2, L0_attn_xp_w2, L0_attn_dtp_w2, L0_attn_dtp_b2, L0_attn_A_log2, L0_attn_Dvec2, L0_attn_out_w2, L0_ffn_gate_w, L0_ffn_wg, L0_ffn_wu, L0_ffn_wd):

    def _L0_attn_ref(x, in_w1, conv_w1, conv_b1, xp_w1, dtp_w1, dtp_b1, A_log1, Dvec1, out_w1, in_w2, conv_w2, conv_b2, xp_w2, dtp_w2, dtp_b2, A_log2, Dvec2, out_w2):
        import jax, jax.numpy as jnp
        import numpy as np
        D_MODEL, D_STATE, D_CONV, EXPAND = (128, 16, 4, 2)
        D_INNER = EXPAND * D_MODEL
        DT_RANK = (D_MODEL + 15) // 16
        B, L = (2, 256)

        def _mamba(x, in_w, conv_w, conv_b, xp_w, dtp_w, dtp_b, A_log, Dp, out_w):
            di = A_log.shape[0]
            n = A_log.shape[1]
            r = dtp_w.shape[1]
            xz = x @ in_w.T
            xi, z = jnp.split(xz, 2, axis=-1)
            xc = jnp.transpose(xi, (0, 2, 1))
            xc = jax.lax.conv_general_dilated(xc, conv_w, window_strides=(1,), padding=[(conv_w.shape[-1] - 1, 0)], dimension_numbers=('NCH', 'OIH', 'NCH'), feature_group_count=di)
            xc = jax.nn.silu(xc + conv_b[None, :, None])
            xc = jnp.transpose(xc, (0, 2, 1))
            x_dbl = xc @ xp_w.T
            dt = x_dbl[..., :r]
            Bm = x_dbl[..., r:r + n]
            Cm = x_dbl[..., r + n:]
            delta = jax.nn.softplus(dt @ dtp_w.T + dtp_b)
            A = -jnp.exp(A_log)

            def step(h, inp):
                u_t, d_t, b_t, c_t = inp
                dA = jnp.exp(d_t[:, :, None] * A)
                h = h * dA + (d_t * u_t)[:, :, None] * b_t[:, None, :]
                y = jnp.einsum('bdn,bn->bd', h, c_t)
                return (h, y)
            h0 = jnp.zeros((x.shape[0], di, n), x.dtype)
            ins = (jnp.transpose(xc, (1, 0, 2)), jnp.transpose(delta, (1, 0, 2)), jnp.transpose(Bm, (1, 0, 2)), jnp.transpose(Cm, (1, 0, 2)))
            _, ys = jax.lax.scan(step, h0, ins)
            y = jnp.transpose(ys, (1, 0, 2)) + xc * Dp
            y = y * jax.nn.silu(z)
            return y @ out_w.T

        def _mamba_params(key):
            ks = jax.random.split(key, 7)
            s = 0.02
            in_w = jax.random.normal(ks[0], (2 * D_INNER, D_MODEL), jnp.float32) * s
            conv_w = jax.random.normal(ks[1], (D_INNER, 1, D_CONV), jnp.float32) * 0.2
            conv_b = jnp.zeros((D_INNER,), jnp.float32)
            xp_w = jax.random.normal(ks[2], (DT_RANK + 2 * D_STATE, D_INNER), jnp.float32) * s
            dtp_w = jax.random.normal(ks[3], (D_INNER, DT_RANK), jnp.float32) * 0.1
            dtp_b = jax.random.normal(ks[4], (D_INNER,), jnp.float32) * 0.1 - 4.0
            A_log = jnp.broadcast_to(jnp.log(jnp.arange(1, D_STATE + 1, dtype=jnp.float32)), (D_INNER, D_STATE)).copy()
            Dp = jnp.ones((D_INNER,), jnp.float32)
            out_w = jax.random.normal(ks[5], (D_MODEL, D_INNER), jnp.float32) * s
            return (in_w, conv_w, conv_b, xp_w, dtp_w, dtp_b, A_log, Dp, out_w)
        y = _mamba(x, in_w1, conv_w1, conv_b1, xp_w1, dtp_w1, dtp_b1, A_log1, Dvec1, out_w1)
        iy = _mamba(jnp.flip(x, axis=1), in_w2, conv_w2, conv_b2, xp_w2, dtp_w2, dtp_b2, A_log2, Dvec2, out_w2)
        return y + iy

    def _L0_ffn_ref(x, gate_w, wg, wu, wd):
        import jax, jax.numpy as jnp
        import numpy as np
        B, S, H = (2, 256, 128)
        E, I, K = (8, 512, 2)

        def _moe_forward(x, gate_w, wg, wu, wd):
            b, s, h = x.shape
            x_flat = x.reshape(-1, h)
            logits = x_flat @ gate_w.T
            top_v, top_i = jax.lax.top_k(logits, K)
            probs = jax.nn.softmax(top_v.astype(jnp.float32), axis=-1).astype(logits.dtype)
            one_hot = jax.nn.one_hot(top_i, E, dtype=probs.dtype)
            combine = jnp.einsum('tk,tke->et', probs, one_hot)

            def body(acc, ws):
                wge, wue, wde, we = ws
                hidden = jax.nn.silu(x_flat @ wge.T) * (x_flat @ wue.T)
                return (acc + we[:, None] * (hidden @ wde.T), None)
            out, _ = jax.lax.scan(body, jnp.zeros_like(x_flat), (wg, wu, wd, combine))
            return out.reshape(b, s, h)
        return _moe_forward(x, gate_w, wg, wu, wd)
    x = L0_attn_x
    x = x + 0.5 * _L0_ffn_ref(_layernorm(x, axis=-1), L0_ffn_gate_w, L0_ffn_wg, L0_ffn_wu, L0_ffn_wd)
    x = x + _L0_attn_ref(_layernorm(x, axis=-1), L0_attn_in_w1, L0_attn_conv_w1, L0_attn_conv_b1, L0_attn_xp_w1, L0_attn_dtp_w1, L0_attn_dtp_b1, L0_attn_A_log1, L0_attn_Dvec1, L0_attn_out_w1, L0_attn_in_w2, L0_attn_conv_w2, L0_attn_conv_b2, L0_attn_xp_w2, L0_attn_dtp_w2, L0_attn_dtp_b2, L0_attn_A_log2, L0_attn_Dvec2, L0_attn_out_w2)
    x = x + 0.5 * _L0_ffn_ref(_layernorm(x, axis=-1), L0_ffn_gate_w, L0_ffn_wg, L0_ffn_wu, L0_ffn_wd)
    return x

_drawn_inputs = setup_inputs


def setup_inputs(seed=0):
    import zlib

    import numpy as np

    out = dict(_drawn_inputs(seed))
    spreads = {'L0_attn_conv_b1': (0.0, 0.1),
     'L0_attn_Dvec1': (1.0, 0.2),
     'L0_attn_conv_b2': (0.0, 0.1),
     'L0_attn_Dvec2': (1.0, 0.2)}
    factors = {}
    for name, (base, spread) in spreads.items():
        noise = np.random.default_rng([zlib.crc32(name.encode()), seed]).standard_normal(out[name].shape)
        drawn = base * np.exp(spread * noise) if base else spread * noise
        out[name] = jnp.asarray(drawn.astype(out[name].dtype))
    for name, factor in factors.items():
        out[name] = (out[name] * factor).astype(out[name].dtype)
    return out
```

```python
from contextlib import ExitStack

import concourse.bass as bass
from concourse import mybir

F32 = mybir.dt.float32
F32R = mybir.dt.float32r
I32 = mybir.dt.int32
U32 = mybir.dt.uint32
ALU = mybir.AluOpType
ACT = mybir.ActivationFunctionType
AX_X = mybir.AxisListType.X
P = 128
DMA = 16
EPS = 1e-5

DVE_PRE = ["stats", "aggr", "vareps", "xn"] + [f"{s}{r}" for r in (0, 1) for s in (
    "tap1c0_", "tap1c1_", "tap2c0_", "tap2c1_", "tap3c0_", "tap3c1_", "lo", "delta", "du")]
ACT_PRE = ["xnT", "xnTrev"] + [f"{s}{r}" for r in (0, 1) for s in (
    "conv0_", "conv1_", "zs0_", "zs1_", "xc", "hi", "dts", "relu0_", "abs0_", "relu1_", "abs1_",
    "exp", "ln")]
PE_PRE = ["xt"] + [f"{s}{r}" for r in (0, 1) for s in (
    "xi0_", "xi1_", "z0_", "z1_", "xdbl", "dt0_", "dt1_")]
DVE_POST = ["skip0", "skip1", "gate", "res"]


def done(steps, name, turn):
    return turn * len(steps) + steps.index(name) + 1


def wait(eng, sem, value):
    if isinstance(value, int) and value <= 0:
        return
    eng.wait_ge(sem, value)


def macaron_kernel(nc, x, gateT, wgT, wuT, wdT, inT, xpT, dtpT, chan, outT, ident, tri, e_rank,
                   e_reset, tile_rank, out):
    T, D = x.shape
    L = 256
    NT = T // P
    NP = T // (2 * L)
    E = gateT.shape[1]
    I = wgT.shape[1] // E
    IC = I // P
    DI = inT.shape[2] // 2
    C = DI // P
    NS = 16
    RK = dtpT.shape[1]
    BC = 2 * NS
    S = 2
    W = S * L
    G = 4
    NG = NT // G
    TILES = -(-(2 * T + E * (P - 1)) // P)
    TILES = -(-TILES // 4) * 4
    assert D == P and C == 2 and I == 512 and W == 512 and NG == NP and NG % 2 == 0
    CONV, CB, DTB, DSK, ALOG = 0, 4, 5, 6, 7

    xs = nc.dram_tensor("slot_rows", [TILES * P, D], F32, kind="Internal").ap()
    ys = nc.dram_tensor("slot_outputs", [TILES * P, D], F32, kind="Internal").ap()

    with ExitStack() as ctx:
        def sb(name, shape, dt=F32):
            return ctx.enter_context(nc.sbuf_tensor(name, shape, dt))

        def sem(name):
            return ctx.enter_context(nc.semaphore(name))

        X = sb("X", [P, NT, D])
        wg_sb = sb("wg_sb", [P, E * I])
        wu_sb = sb("wu_sb", [P, E * I])
        wd_sb = sb("wd_sb", [P, E * IC, D])
        gate_sb = sb("gate_sb", [P, E])
        in_sb = sb("in_sb", [P, 2, 2 * DI])
        xp_sb = sb("xp_sb", [P, 2, C, 2 * BC + RK])
        dtp_sb = sb("dtp_sb", [2 * BC + RK, 2, DI])
        out_sb = sb("out_sb", [P, 2, C, D])
        ch = sb("ch", [P, 2, C, ALOG + NS])
        negA = sb("negA", [P, 2, C, NS])
        id_sb = sb("id_sb", [P, P])
        tri_sb = sb("tri_sb", [P, P])
        ones_sb = sb("ones_sb", [P, P])
        half = sb("half", [P, NT])
        sel = sb("sel", [2 * BC, BC], F32R)
        work = sb("work", [P, 8 * C * W])
        rowsN = work[:, 0:2 * G * D].rearrange("p (b t d) -> p b t d", t=G, d=D)
        unit = [work[:, k * C * W:(k + 1) * C * W] for k in range(8)]
        MV = sb("MV", [P, G, 2])
        st = sb("st", [P, G, 6])
        ve = sb("ve", [P, NT])
        rs = sb("rs", [P, NT])
        ST = sb("ST", [P, NT, 6])
        mean = sb("mean", [P, NT])
        LG = sb("LG", [P, NT, E])
        best = sb("best", [P, 2, NT])
        wt = sb("wt", [P, 2, NT])
        rank_sb = sb("rank_sb", [P, E])
        er_sb = sb("er_sb", [P, E * NT])
        tn_sb = sb("tn_sb", [1, TILES])
        I1 = sb("I1", [P, 2, NT])
        O12 = sb("O12", [P, 2, E, NT])
        MK = sb("MK", [P, E, NT])
        CS = sb("CS", [P, E * NT])
        cnt = sb("cnt", [P, 4, E])
        cnti = sb("cnti", [P, 2, E], I32)
        SLf = sb("SLf", [P, 2, NT])
        SL = sb("SL", [P, NT, 2], U32)
        tc8 = sb("tc8", [1, TILES, E])
        tef = sb("tef", [1, TILES])
        te = sb("te", [1, TILES], I32)
        BUF = max(15 * 512, 7 * 1024 + 9 * 512)
        buf = sb("buf", [P, BUF])

        def carve(at, n):
            return buf[:, at:at + n]

        xin = carve(0, 4 * D).rearrange("p (b d) -> p b d", d=D)
        xT = carve(512, 4 * P).rearrange("p (b d) -> p b d", d=P)
        sg = carve(1024, 2 * I).rearrange("p (b d) -> p b d", d=I)
        hid = carve(2048, 2 * I).rearrange("p (b d) -> p b d", d=I)
        hT = carve(3072, 2 * I).rearrange("p (b d) -> p b d", d=I)
        yo = carve(4096, 4 * D).rearrange("p (b d) -> p b d", d=D)
        rowsA = carve(4608, 2 * G * D).rearrange("p (b t d) -> p b t d", t=G, d=D)
        rowsB = carve(5632, 2 * G * D).rearrange("p (b t d) -> p b t d", t=G, d=D)
        xnTr = carve(6656, 2 * G * P).rearrange("p (b d) -> p b d", d=G * P)
        ZERO = 2048
        zero = carve(4608, ZERO)
        ZEROED = -(-TILES // (ZERO // D)) * DMA
        idx = sb("idx", [P, 2, 2 * G], U32)

        dA = carve(0, 4 * W).rearrange("p (b c s t) -> p b c s t", b=2, c=C, s=S)
        hs = carve(2048, 4 * W).rearrange("p (b w) -> p b w", b=2)
        hC = carve(4096, 4 * W).rearrange("p (b w) -> p b w", b=2)
        Cs = carve(6144, 2 * W).rearrange("p (b w) -> p b w", b=2)
        aex = carve(7168, 2 * W)
        xnT = carve(8192, 2 * W).rearrange("p (b s t) -> p b s t", b=2, s=S)
        gat = carve(9216, 2 * W)
        xn4 = carve(10240, W).rearrange("p (t d) -> p t d", d=D)
        BCs = [sb(f"BCs{r}", [2 * BC, W], F32R) for r in (0, 1)]
        dts = carve(10752, W)
        xc = [unit[0], unit[4]]
        zs = [unit[1], unit[5]]
        delta = [unit[2], unit[6]]
        du = [unit[3], unit[7]]

        bank = [ctx.enter_context(nc.psum_tensor(f"bank{i}", [P, 512], F32)) for i in range(8)]

        names = """scatter_turn gather_turn aggr_turn loaded_x loaded_w zeroed consts stats_done vareps_done rstd_done xn_done
            xt_done xnT_done logit_done logits_act route_dve route_pe route_act stage_done scat0 scat1
            xin0 xin1 xin2 xin3 st0 st1 st2 st3 slotT_pe slotT_act gate_pe up_pe silu_act hid_dve
            hidT_pe hidT_act down_pe yo_act gath0 gath1 comb_done comb_first idx_done stored diff_done mask_done slots_done experts_done expA_done
            dve_pre act_pre pe_pre rstd_pre dve_post pe_post negA_done
            bcB_ready bcC_ready dA_ready mul_done scan_done Cs_ready hC_ready y_done""".split()
        s = {n: sem(n) for n in names}
        block = ctx.enter_context(nc.Block())

        NITER = NG // 2
        @block.sync
        def _(sp):
            sp.dma_start(X[:, :, :], x.rearrange("(t p) d -> p t d", p=P)).then_inc(s["loaded_x"], DMA)
            small = [(id_sb[:, :], ident), (tri_sb[:, :], tri), (gate_sb[:, :], gateT),
                     (rank_sb[:, :], e_rank), (er_sb[:, :], e_reset), (tn_sb[:, :], tile_rank),
                     (in_sb[:, :, :], inT.rearrange("r p n -> p r n")),
                     (xp_sb[:, :, :, :], xpT.rearrange("r p c n -> p r c n")),
                     (dtp_sb[2 * BC:, :, :], dtpT.rearrange("r k n -> k r n")),
                     (ch[:, :, :, :], chan.rearrange("r p c n -> p r c n")),
                     (out_sb[:, :, :, :], outT.rearrange("r p c n -> p r c n")),
                     (wg_sb[:, :], wgT), (wu_sb[:, :], wuT), (wd_sb[:, :, :], wdT)]
            for dst, src in small:
                sp.dma_start(dst, src).then_inc(s["loaded_w"], DMA)

            def load_slots(m, i, b):
                wait(sp, s["slotT_pe"], m * TILES + i - 3)
                sp.dma_start(xin[:, b, :], xs[bass.ds(i * P, P), :]).then_inc(s[f"xin{b}"], DMA)

            def experts(m):
                sp.wait_ge(s["scat0"], (m + 1) * NG // 2 * 2 * G * DMA)
                sp.wait_ge(s["scat1"], (m + 1) * NG // 2 * 2 * G * DMA)
                for i in range(4):
                    load_slots(m, i, i)

                def store(i, b):
                    sp.wait_ge(s["yo_act"], m * TILES + i + 1)
                    sp.dma_start(ys[bass.ds(i * P, P), :], yo[:, b, :]).then_inc(s[f"st{b}"], DMA)

                with sp.Fori(0, TILES // 4 - 1) as k:
                    for b in range(4):
                        load_slots(m, k * 4 + 4 + b, b)
                        store(k * 4 + b, b)
                for b in range(4):
                    store(TILES - 4 + b, b)

            experts(0)
            experts(1)
            for g in range(NG):
                sp.wait_ge(s["comb_done"], NG + g + 1)
                sp.dma_start(out[g * G * P:(g + 1) * G * P, :].rearrange("(t p) d -> p t d", p=P),
                             X[:, g * G:(g + 1) * G, :]).then_inc(s["stored"], DMA)
            sp.wait_ge(s["stored"], NG * DMA)

        @block.gpsimd
        def _(pool):
            pool.memset(ones_sb[:, :], 1.0).then_inc(s["consts"], 1)
            pool.memset(half[:, :], -0.5).then_inc(s["consts"], 1)
            pool.memset(zero, 0.0).then_inc(s["consts"], 1)
            pool.wait_ge(s["consts"], 3)
            ZT = ZERO // D
            for a in range(0, TILES, ZT):
                n = min(ZT, TILES - a)
                pool.dma_start(xs[a * P:(a + n) * P, :].rearrange("(t p) d -> p t d", p=P),
                               zero[:, 0:n * D].rearrange("p (t d) -> p t d", d=D)).then_inc(s["zeroed"], DMA)

            def moe(m):
                if m == 0:
                    pool.wait_ge(s["zeroed"], ZEROED)
                pool.wait_ge(s["vareps_done"], m + 1)
                pool.tensor_tensor(rs[:, :], ve[:, :], half[:, :], ALU.pow).then_inc(s["rstd_done"], 1)

                def scatter(g, b):
                    pool.wait_ge(s["stage_done"], m * NG + g + 1)
                    pool.sem_inc(s["scatter_turn"], 1)
                    for t in range(G):
                        for k in range(2):
                            pool.indirect_dma_start(
                                out=xs[:, :], out_offset=bass.IndirectOffsetOnAxis(
                                    ap=idx[:, b, 2 * t + k:2 * t + k + 1], axis=0),
                                in_=rowsA[:, b, t, :], in_offset=None).then_inc(s[f"scat{b}"], DMA)

                with pool.Fori(0, NITER) as i:
                    for b in range(2):
                        scatter(i * 2 + b, b)

                for b in range(4):
                    pool.wait_ge(s[f"st{b}"], (m + 1) * TILES // 4 * DMA)

                def gather(g, b):
                    pool.wait_ge(s["idx_done"], m * NG + g + 1)
                    wait(pool, s["comb_done"], m * NG + g - 1)
                    pool.sem_inc(s["gather_turn"], 1)
                    for t in range(G):
                        for k, rows in ((0, rowsA), (1, rowsB)):
                            pool.indirect_dma_start(
                                out=rows[:, b, t, :], out_offset=None, in_=ys[:, :],
                                in_offset=bass.IndirectOffsetOnAxis(
                                    ap=idx[:, b, 2 * t + k:2 * t + k + 1], axis=0)).then_inc(s[f"gath{b}"], DMA)

                for b in range(2):
                    gather(b, b)
                with pool.Fori(1, NITER) as i:
                    for b in range(2):
                        gather(i * 2 + b, b)

            moe(0)

            def rstd(p):
                pool.wait_ge(s["dve_pre"], done(DVE_PRE, "vareps", p))
                pool.tensor_tensor(rs[:, 0:G], ve[:, 0:G], half[:, 0:G], ALU.pow).then_inc(s["rstd_pre"], 1)

            def pair(p, first, last):
                for r in range(2):
                    for n in range(NS):
                        N = p * 2 * NS + r * NS + n
                        b = n % 2
                        pool.wait_ge(s["scan_done"], 2 * N + 2)
                        pool.wait_ge(s["Cs_ready"], N + 1)
                        wait(pool, s["y_done"], N - 1)
                        pool.tensor_tensor(hC[:, b, :].rearrange("p (c w) -> p c w", c=C),
                                           hs[:, b, :].rearrange("p (c w) -> p c w", c=C),
                                           Cs[:, b, :].unsqueeze(1).broadcast_to([P, C, W]),
                                           ALU.mult).then_inc(s["hC_ready"], 1)
                        if r == 1 and n == 3 and not last:
                            rstd(p + 1)

            rstd(0)
            pair(0, True, False)
            with pool.Fori(1, NP - 1) as p:
                pair(p, False, False)
            pair(NP - 1, False, True)
            moe(1)

        @block.vector
        def _(dve):
            V = nc.vector
            seq = [0]

            def chain(ins, name="route_dve", count=0):
                if name == "route_dve":
                    seq[0] += 1
                    count = seq[0]
                ins.then_inc(s[name], 1)
                dve.wait_ge(s[name], count)

            dve.wait_ge(s["loaded_w"], 14 * DMA)
            dve.wait_ge(s["loaded_x"], DMA)
            dve.wait_ge(s["consts"], 3)
            V.tensor_copy(sel[0:BC, :], id_sb[0:BC, 0:BC])
            chain(V.tensor_copy(sel[BC:2 * BC, :], id_sb[BC:2 * BC, BC:2 * BC]))

            def moe(m):
                def stats(g):
                    for t in range(G):
                        ins = V.bn_stats(ST[:, bass.ds(g * G + t, 1), :], X[:, bass.ds(g * G + t, 1), :])
                    ins.then_inc(s["stats_done"], 1)

                with dve.Fori(0, NG) as g:
                    stats(g)
                dve.wait_ge(s["stats_done"], (m + 1) * NG)
                chain(V.tensor_tensor(mean[:, :], ST[:, :, 1], ST[:, :, 4], ALU.add))
                chain(V.tensor_tensor(ve[:, :], ST[:, :, 1], ST[:, :, 4], ALU.subtract))
                chain(V.tensor_scalar(mean[:, :], mean[:, :], 0.5, None, ALU.mult))
                chain(V.scalar_tensor_tensor(out=ve[:, :], in0=ve[:, :], scalar=0.25, in1=ve[:, :],
                                             op0=ALU.mult, op1=ALU.mult))
                chain(V.tensor_tensor(rs[:, :], ST[:, :, 2], ST[:, :, 5], ALU.add))
                chain(V.scalar_tensor_tensor(out=ve[:, :], in0=rs[:, :], scalar=1.0 / D, in1=ve[:, :],
                                             op0=ALU.mult, op1=ALU.add))
                V.tensor_scalar(ve[:, :], ve[:, :], EPS, None, ALU.add).then_inc(s["vareps_done"], 1)
                dve.wait_ge(s["rstd_done"], m + 1)

                def normalise(g, rows):
                    for t in range(G):
                        ins = V.tensor_scalar(rows[:, t:t + 1, :], X[:, bass.ds(g * G + t, 1), :],
                                              mean[:, bass.ds(g * G + t, 1)], rs[:, bass.ds(g * G + t, 1)],
                                              ALU.subtract, ALU.mult)
                    return ins

                def normalise_for_logits(g, b):
                    wait(dve, s["xt_done"], m * NG + g - 1)
                    normalise(g, rowsN[:, b, :, :]).then_inc(s["xn_done"], 1)

                for b in range(2):
                    normalise_for_logits(b, b)
                with dve.Fori(1, NITER) as i:
                    for b in range(2):
                        normalise_for_logits(i * 2 + b, b)
                dve.wait_ge(s["logits_act"], (m + 1) * NG)

                LGe = LG[:, :, :].rearrange("p t e -> p e t")
                for k in range(2):
                    one = O12[:, k, :, :]
                    chain(V.tensor_reduce(best[:, k, :], LG[:, :, :], AX_X, ALU.max))
                    chain(V.tensor_tensor(one, LGe, best[:, k, :].unsqueeze(1).broadcast_to([P, E, NT]),
                                          ALU.is_equal))
                    chain(V.tensor_tensor(one, one, rank_sb[:, :].unsqueeze(2).broadcast_to([P, E, NT]), ALU.mult))
                    chain(V.tensor_reduce(I1[:, k, :], one.rearrange("p e t -> p t e"), AX_X, ALU.max))
                    chain(V.tensor_tensor(one, rank_sb[:, :].unsqueeze(2).broadcast_to([P, E, NT]),
                                          I1[:, k, :].unsqueeze(1).broadcast_to([P, E, NT]), ALU.is_equal))
                    if k == 0:
                        chain(V.scalar_tensor_tensor(out=LG[:, :, :], in0=one.rearrange("p e t -> p t e"),
                                                     scalar=-3e38, in1=LG[:, :, :], op0=ALU.mult, op1=ALU.add))
                chain(V.tensor_tensor(MK[:, :, :], O12[:, 0, :, :], O12[:, 1, :, :], ALU.add), "mask_done", m + 1)

                chain(V.tensor_tensor(SLf[:, 0, :], best[:, 1, :], best[:, 0, :], ALU.subtract), "diff_done", m + 1)
                dve.wait_ge(s["route_act"], m + 1)
                chain(V.tensor_scalar(SLf[:, 0, :], SLf[:, 1, :], 1.0, None, ALU.add))
                chain(V.reciprocal(SLf[:, 0, :], SLf[:, 0, :]))
                chain(V.tensor_scalar(wt[:, 0, :], SLf[:, 0, :], 0.5, None, ALU.mult))
                chain(V.tensor_tensor(wt[:, 1, :], wt[:, 0, :], SLf[:, 1, :], ALU.mult))
                dve.wait_ge(s["route_pe"], 2 * m + 2)
                tot = bank[7][:, 0:E * NT]
                chain(V.tensor_tensor_scan(CS[:, :], er_sb[:, :], tot, 0.0, ALU.mult, ALU.add))
                CS3 = CS[:, :].rearrange("p (e t) -> p e t", e=E)
                chain(V.tensor_scalar(cnti[:, 0, :], CS3[:, :, NT - 1], float(P - 1), None, ALU.add))
                chain(V.tensor_scalar(cnti[:, 1, :], cnti[:, 0, :], 7, None, ALU.logical_shift_right))
                chain(V.tensor_copy(cnt[:, 0, :], cnti[:, 1, :]))
                chain(V.tensor_tensor_scan(cnt[:, 1, :], ones_sb[:, 0:E], cnt[:, 0, :], 0.0, ALU.mult, ALU.add))
                chain(V.tensor_tensor(cnt[:, 2, :], cnt[:, 1, :], cnt[:, 0, :], ALU.subtract))
                chain(V.tensor_scalar(cnt[:, 3, :], cnt[:, 2, :], float(P), None, ALU.mult))
                chain(V.tensor_tensor(CS[:, :], CS[:, :], tot, ALU.subtract))
                chain(V.tensor_tensor(CS[:, :], CS[:, :], bank[6][:, 0:E * NT], ALU.add))
                chain(V.tensor_tensor(CS3, CS3, cnt[:, 3, :].unsqueeze(2).broadcast_to([P, E, NT]), ALU.add))
                for k in range(2):
                    chain(V.tensor_tensor(O12[:, k, :, :], O12[:, k, :, :], CS3, ALU.mult))
                    chain(V.tensor_reduce(SLf[:, k, :], O12[:, k, :, :].rearrange("p e t -> p t e"), AX_X, ALU.add))
                chain(V.tensor_copy(SL[:, :, :], SLf[:, :, :].rearrange("p k t -> p t k")), "slots_done", m + 1)
                chain(V.tensor_tensor(tc8[:, :, :], tn_sb[:, :].unsqueeze(2).broadcast_to([1, TILES, E]),
                                      cnt[0:1, 1, :].unsqueeze(1).broadcast_to([1, TILES, E]), ALU.is_ge))
                chain(V.tensor_reduce(tef[:, :], tc8[:, :, :], AX_X, ALU.add))
                chain(V.tensor_scalar(te[:, :], tef[:, :], float(E - 1), None, ALU.min), "experts_done", m + 1)

                dve.wait_ge(s["zeroed"], ZEROED)

                def stage(g, b, k):
                    wait(dve, s[f"scat{b}"], (m * NITER + k) * 2 * G * DMA)
                    normalise(g, rowsA[:, b, :, :])
                    V.tensor_copy(idx[:, b, :], SL[:, bass.ds(g * G, G), :].rearrange("p t k -> p (t k)")
                                  ).then_inc(s["stage_done"], 1)

                for b in range(2):
                    stage(b, b, 0)
                with dve.Fori(1, NITER) as i:
                    for b in range(2):
                        stage(i * 2 + b, b, i)

                def hidden(i, b):
                    dve.wait_ge(s["silu_act"], m * TILES + i + 1)
                    dve.wait_ge(s["up_pe"], m * TILES + i + 1)
                    wait(dve, s["hidT_pe"], m * TILES + i - 1)
                    V.tensor_tensor(hid[:, b, :], sg[:, b, :], bank[2 + b][:, :], ALU.mult).then_inc(s["hid_dve"], 1)

                hidden(0, 0)
                hidden(1, 1)
                with dve.Fori(1, TILES // 2) as k:
                    for b in range(2):
                        hidden(k * 2 + b, b)

                def combine(g, b, k):
                    dve.wait_ge(s[f"gath{b}"], (m * NITER + k + 1) * 2 * G * DMA)
                    for w, rows in ((0, rowsA), (1, rowsB)):
                        for t in range(G):
                            xt = X[:, bass.ds(g * G + t, 1), :]
                            ins = V.scalar_tensor_tensor(out=xt, in0=rows[:, b, t:t + 1, :],
                                                         scalar=wt[:, w, bass.ds(g * G + t, 1)],
                                                         in1=xt, op0=ALU.mult, op1=ALU.add)
                        if w == 0:
                            ins.then_inc(s["comb_first"], 1)
                            dve.wait_ge(s["comb_first"], m * NG + g + 1)
                    ins.then_inc(s["comb_done"], 1)

                with dve.Fori(0, NITER) as i:
                    for b in range(2):
                        combine(i * 2 + b, b, i)
                dve.wait_ge(s["comb_done"], (m + 1) * NG)

            moe(0)

            dve.wait_ge(s["expA_done"], 1)
            V.tensor_scalar(negA[:, :, :, :], negA[:, :, :, :], -1.0, None, ALU.mult).then_inc(s["negA_done"], 1)
            dve.wait_ge(s["yo_act"], TILES)
            chain(V.memset(dA[:, :, :, :, 0:1], 0.0))

            def step_done(name, turn):
                dve.wait_ge(s["dve_pre"], done(DVE_PRE, name, turn))

            def layernorm(p):
                wait(dve, s["dve_pre"], done(DVE_PRE, "xn", p - 1))
                for t in range(G):
                    ins = V.bn_stats(st[:, t, :], X[:, bass.ds(p * G + t, 1), :])
                ins.then_inc(s["dve_pre"], 1)
                step_done("stats", p)
                dve.sem_inc(s["aggr_turn"], 1)
                for t in range(G):
                    ins = V.bn_aggr(MV[:, t, :], st[:, t, :])
                ins.then_inc(s["dve_pre"], 1)
                step_done("aggr", p)
                V.tensor_scalar(ve[:, 0:G], MV[:, :, 1], EPS, None, ALU.add).then_inc(s["dve_pre"], 1)

            def normalise(p):
                dve.wait_ge(s["rstd_pre"], p + 1)
                wait(dve, s["pe_pre"], done(PE_PRE, "xt", p - 1))
                for t in range(G):
                    ins = V.tensor_scalar(xn4[:, t, :], X[:, bass.ds(p * G + t, 1), :], MV[:, t, 0:1],
                                          rs[:, t:t + 1], ALU.subtract, ALU.mult)
                ins.then_inc(s["dve_pre"], 1)

            def taps(p, r, j):
                for c in range(C):
                    acc = xc[r].rearrange("p (c s t) -> p c s t", c=C, s=S)[:, c, :, j:]
                    xi = bank[6 + c][:, :].rearrange("p (s t) -> p s t", s=S)[:, :, 0:L - j]
                    if j == 1:
                        dve.wait_ge(s["act_pre"], done(ACT_PRE, f"conv1_{r}", p))
                    else:
                        step_done(f"tap{j - 1}c{c}_{r}", p)
                    V.scalar_tensor_tensor(out=acc, in0=xi, scalar=ch[:, r, c, 3 - j:4 - j], in1=acc,
                                           op0=ALU.mult, op1=ALU.add).then_inc(s["dve_pre"], 1)

            def split_lo(p, r):
                dve.wait_ge(s["act_pre"], done(ACT_PRE, f"dts{r}", p))
                V.tensor_tensor(BCs[r][BC:2 * BC, :], bank[6][BC:2 * BC, :], BCs[r][BC:2 * BC, :].bitcast(F32),
                                ALU.subtract).then_inc(s["dve_pre"], 1)

            def step_size(p, r):
                dve.wait_ge(s["act_pre"], done(ACT_PRE, f"ln{r}", p))
                V.tensor_tensor(delta[r], delta[r], aex, ALU.add).then_inc(s["dve_pre"], 1)
                step_done(f"delta{r}", p)
                V.tensor_tensor(du[r], delta[r], xc[r], ALU.mult).then_inc(s["dve_pre"], 1)

            def post_gate(u, r):
                dve.wait_ge(s["y_done"], (u + 1) * NS)
                wait(dve, s["pe_post"], u)
                for c in range(C):
                    V.scalar_tensor_tensor(out=gat[:, c * W:(c + 1) * W], in0=xc[r][:, c * W:(c + 1) * W],
                                           scalar=ch[:, r, c, DSK:DSK + 1], in1=bank[4 + c][:, :],
                                           op0=ALU.mult, op1=ALU.add).then_inc(s["dve_post"], 1)
                dve.wait_ge(s["dve_post"], done(DVE_POST, "skip1", u))
                V.tensor_tensor(gat, gat, zs[r], ALU.mult).then_inc(s["dve_post"], 1)

            def post_residual(u, p, r):
                dve.wait_ge(s["pe_post"], u + 1)
                xp4 = X[:, bass.ds(p * G, G), :]
                V.tensor_tensor(xp4, xp4, bank[6][:, :].rearrange("p (t d) -> p t d", t=G),
                                ALU.add).then_inc(s["dve_post"], 1)

            def scan_step(p, r, n):
                N = p * 2 * NS + r * NS + n
                b = n % 2
                for c in range(C):
                    if c == 0:
                        dve.wait_ge(s["bcB_ready"], N + 1)
                    wait(dve, s["scan_done"], N * 2 - 1 + c)
                    V.tensor_tensor(bank[c][:, :], du[r][:, c * W:(c + 1) * W], bank[2][:, :],
                                    ALU.mult).then_inc(s["mul_done"], 1)
                for c in range(C):
                    if c == 0:
                        dve.wait_ge(s["dA_ready"], N + 1)
                        wait(dve, s["hC_ready"], N - 1)
                    dve.wait_ge(s["mul_done"], N * 2 + c + 1)
                    V.tensor_tensor_scan(hs[:, b, c * W:(c + 1) * W],
                                         dA[:, b, c, :, :].rearrange("p s t -> p (s t)"),
                                         bank[c][:, :], 0.0, ALU.mult, ALU.add).then_inc(s["scan_done"], 1)

            def pair(p, first, last):
                for r in range(2):
                    u = p * 2 + r
                    pv, rv = (p, 1) if r == 0 else (p + 1, 0)
                    prep = not (last and r == 1)
                    for n in range(NS):
                        if n == 0:
                            dve.wait_ge(s["dve_pre"], done(DVE_PRE, f"du{r}", p))
                        scan_step(p, r, n)
                        if n == 0 and not (first and r == 0):
                            post_gate(u - 1, 1 - r)
                        if n == 2 and not (first and r == 0):
                            post_residual(u - 1, p - 1 if r == 0 else p, 1 - r)
                        if not prep:
                            continue
                        if n == 3 and rv == 0:
                            layernorm(pv)
                        if n == 4 and rv == 0:
                            normalise(pv)
                        if n in (7, 8, 9):
                            taps(pv, rv, n - 6)
                        if n == 13:
                            split_lo(pv, rv)
                        if n == 15:
                            step_size(pv, rv)

            layernorm(0)
            normalise(0)
            for j in (1, 2, 3):
                taps(0, 0, j)
            split_lo(0, 0)
            step_size(0, 0)
            pair(0, True, False)
            with dve.Fori(1, NP - 1) as p:
                pair(p, False, False)
            pair(NP - 1, False, True)
            post_gate(2 * NP - 1, 1)
            post_residual(2 * NP - 1, NP - 1, 1)
            dve.wait_ge(s["dve_post"], done(DVE_POST, "res", 2 * NP - 1))
            moe(1)

        @block.scalar
        def _(act):
            A = nc.scalar
            act.wait_ge(s["loaded_w"], 14 * DMA)
            A.activation(negA[:, :, :, :], ch[:, :, :, ALOG:ALOG + NS], ACT.Exp).then_inc(s["expA_done"], 1)

            def moe(m):
                def evacuate(g, b):
                    act.wait_ge(s["xt_done"], m * NG + g + 1)
                    wait(act, s["logit_done"], m * NG + g - 1)
                    A.activation(xnTr[:, b, :], bank[b][:, :], ACT.Copy).then_inc(s["xnT_done"], 1)

                def copy_logits(g, b):
                    act.wait_ge(s["logit_done"], m * NG + g + 1)
                    A.activation(LG[:, bass.ds(g * G, G), :], bank[4 + b][:, 0:G * E].rearrange("p (t e) -> p t e", e=E),
                                 ACT.Copy).then_inc(s["logits_act"], 1)

                evacuate(0, 0)
                for b in range(2):
                    evacuate(b + 1, 1 - b)
                    copy_logits(b, b)
                with act.Fori(1, NITER - 1) as i:
                    for b in range(2):
                        evacuate(i * 2 + b + 1, 1 - b)
                        copy_logits(i * 2 + b, b)
                evacuate(NG - 1, 1)
                copy_logits(NG - 2, 0)
                copy_logits(NG - 1, 1)
                act.wait_ge(s["diff_done"], m + 1)
                A.activation(SLf[:, 1, :], SLf[:, 0, :], ACT.Exp).then_inc(s["route_act"], 1)

                def copy_slotT(i, b):
                    act.wait_ge(s["slotT_pe"], m * TILES + i + 1)
                    wait(act, s["up_pe"], m * TILES + i - 1)
                    A.activation(xT[:, b, :], bank[4][:, 0:P], ACT.Copy).then_inc(s["slotT_act"], 1)

                def silu(i, b):
                    act.wait_ge(s["gate_pe"], m * TILES + i + 1)
                    wait(act, s["hid_dve"], m * TILES + i - 1)
                    A.activation(sg[:, b, :], bank[b][:, :], ACT.Silu).then_inc(s["silu_act"], 1)

                def copy_hidT(i, b):
                    act.wait_ge(s["hidT_pe"], m * TILES + i + 1)
                    wait(act, s["down_pe"], m * TILES + i - 1)
                    A.activation(hT[:, b, :], bank[5][:, :], ACT.Copy).then_inc(s["hidT_act"], 1)

                def copy_out(i, b2, k):
                    act.wait_ge(s["down_pe"], m * TILES + i + 1)
                    wait(act, s[f"st{b2}"], (m * (TILES // 4) + k) * DMA)
                    A.activation(yo[:, b2, :], bank[6][:, 0:D], ACT.Copy).then_inc(s["yo_act"], 1)

                def tile(i, q, k):
                    if not (isinstance(i, int) and i == TILES - 1):
                        copy_slotT(i + 1, (q + 1) % 2)
                    silu(i, q % 2)
                    if not (isinstance(i, int) and i == 0):
                        copy_hidT(i - 1, (q - 1) % 2)
                        copy_out(i - 1, (q - 1) % 4, k if q else k - 1)

                copy_slotT(0, 0)
                for q in range(4):
                    tile(q, q, 0)
                with act.Fori(1, TILES // 4 - 1) as k:
                    for q in range(4):
                        tile(k * 4 + q, q, k)
                for q in range(4):
                    tile(TILES - 4 + q, q, TILES // 4 - 1)
                copy_hidT(TILES - 1, 1)
                copy_out(TILES - 1, 3, TILES // 4 - 1)

                def stage_idx(g, b, k):
                    if isinstance(k, int) and k == 0:
                        act.wait_ge(s[f"scat{b}"], (m + 1) * NITER * 2 * G * DMA)
                    else:
                        act.wait_ge(s[f"gath{b}"], (m * NITER + k) * 2 * G * DMA)
                    A.activation(idx[:, b, :], SL[:, bass.ds(g * G, G), :].rearrange("p t k -> p (t k)"),
                                 ACT.Copy).then_inc(s["idx_done"], 1)

                for b in range(2):
                    stage_idx(b, b, 0)
                with act.Fori(1, NITER) as i:
                    for b in range(2):
                        stage_idx(i * 2 + b, b, i)

            moe(0)
            act.wait_ge(s["comb_done"], NG)
            act.wait_ge(s["negA_done"], 1)

            def step(ins):
                ins.then_inc(s["act_pre"], 1)

            def normT(p):
                act.wait_ge(s["pe_pre"], done(PE_PRE, "xt", p))
                wait(act, s["pe_pre"], done(PE_PRE, "z1_1", p - 1))
                src = bank[6][:, :].rearrange("p (s t) -> p s t", s=S)
                step(A.activation(xnT[:, 0, :, :], src, ACT.Copy))
                step(A.activation(xnT[:, 1, :, ::-1], src, ACT.Copy))

            def conv_start(p, r):
                for c in range(C):
                    act.wait_ge(s["pe_pre"], done(PE_PRE, f"xi{c}_{r}", p))
                    step(A.activation(xc[r][:, c * W:(c + 1) * W], bank[6 + c][:, :], ACT.Identity,
                                      bias=ch[:, r, c, CB:CB + 1], scale=ch[:, r, c, 3:4]))

            def silus(p, r):
                for c in range(C):
                    act.wait_ge(s["pe_pre"], done(PE_PRE, f"z{c}_{r}", p))
                    step(A.activation(zs[r][:, c * W:(c + 1) * W], bank[6 + c][:, :], ACT.Silu))
                act.wait_ge(s["dve_pre"], done(DVE_PRE, f"tap3c1_{r}", p))
                step(A.activation(xc[r], xc[r], ACT.Silu))

            def split_hi(p, r):
                act.wait_ge(s["pe_pre"], done(PE_PRE, f"xdbl{r}", p))
                step(A.activation(BCs[r][:, :], bank[6][0:2 * BC, :], ACT.Copy))
                step(A.activation(dts[2 * BC:2 * BC + RK, :], bank[6][2 * BC:2 * BC + RK, :], ACT.Copy))

            def softplus_parts(p, r):
                for c, bk in ((0, bank[7]), (1, bank[6])):
                    act.wait_ge(s["pe_pre"], done(PE_PRE, f"dt{c}_{r}", p))
                    step(A.activation(delta[r][:, c * W:(c + 1) * W], bk[:, :], ACT.Relu,
                                      bias=ch[:, r, c, DTB:DTB + 1]))
                    if c == 0:
                        wait(act, s["dve_pre"], done(DVE_PRE, "delta0", p) if r else done(DVE_PRE, "delta1", p - 1))
                    step(A.activation(aex[:, c * W:(c + 1) * W], bk[:, :], ACT.Abs,
                                      bias=ch[:, r, c, DTB:DTB + 1]))

            def log1pexp(p, r):
                act.wait_ge(s["act_pre"], done(ACT_PRE, f"abs1_{r}", p))
                step(A.activation(aex, aex, ACT.Exp, scale=-1.0))
                act.wait_ge(s["act_pre"], done(ACT_PRE, f"exp{r}", p))
                step(A.activation(aex, aex, ACT.Ln, bias=1.0))

            def decay_step(p, r, n):
                N = p * 2 * NS + r * NS + n
                b = n % 2
                wait(act, s["scan_done"], N * 2 - 2)
                if n == 0:
                    act.wait_ge(s["dve_pre"], done(DVE_PRE, f"delta{r}", p))
                for c in range(C):
                    ins = A.activation(dA[:, b, c, :, 1:],
                                       delta[r][:, c * W:(c + 1) * W].rearrange("p (s t) -> p s t", s=S)[:, :, 1:],
                                       ACT.Exp, scale=negA[:, r, c, n:n + 1])
                ins.then_inc(s["dA_ready"], 1)
                act.wait_ge(s["bcC_ready"], N + 1)
                wait(act, s["hC_ready"], N - 1)
                A.activation(Cs[:, b, :], bank[3][:, :], ACT.Copy).then_inc(s["Cs_ready"], 1)

            def pair(p, first, last):
                for r in range(2):
                    pv, rv = (p, 1) if r == 0 else (p + 1, 0)
                    prep = not (last and r == 1)
                    for n in range(NS):
                        decay_step(p, r, n)
                        if not prep:
                            continue
                        if n == 5 and rv == 0:
                            normT(pv)
                        if n == 6:
                            conv_start(pv, rv)
                        if n == 11:
                            silus(pv, rv)
                        if n == 12:
                            split_hi(pv, rv)
                        if n == 14:
                            softplus_parts(pv, rv)
                            log1pexp(pv, rv)

            normT(0)
            conv_start(0, 0)
            silus(0, 0)
            split_hi(0, 0)
            softplus_parts(0, 0)
            log1pexp(0, 0)
            pair(0, True, False)
            with act.Fori(1, NP - 1) as p:
                pair(p, False, False)
            pair(NP - 1, False, True)
            act.wait_ge(s["y_done"], 2 * NP * NS)
            act.wait_ge(s["dve_post"], done(DVE_POST, "res", 2 * NP - 1))
            moe(1)

        @block.tensor
        def _(pe):
            M = nc.tensor
            pe.wait_ge(s["loaded_w"], 14 * DMA)
            pe.wait_ge(s["consts"], 3)

            def moe(m):
                def turn(g, b):
                    pe.wait_ge(s["xn_done"], m * NG + g + 1)
                    wait(pe, s["xnT_done"], m * NG + g - 1)
                    for t in range(G):
                        ins = M.transpose(bank[b][:, t * P:(t + 1) * P], rowsN[:, b, t, :], id_sb[:, :])
                    ins.then_inc(s["xt_done"], 1)

                def logits(g, b):
                    pe.wait_ge(s["xnT_done"], m * NG + g + 1)
                    wait(pe, s["logits_act"], m * NG + g - 1)
                    for t in range(G):
                        ins = M.matmul(bank[4 + b][:, t * E:(t + 1) * E], xnTr[:, b, t * P:(t + 1) * P],
                                       gate_sb[:, :], start=True, stop=True)
                    ins.then_inc(s["logit_done"], 1)

                turn(0, 0)
                for b in range(2):
                    turn(b + 1, 1 - b)
                    logits(b, b)
                with pe.Fori(1, NITER - 1) as i:
                    for b in range(2):
                        turn(i * 2 + b + 1, 1 - b)
                        logits(i * 2 + b, b)
                turn(NG - 1, 1)
                logits(NG - 2, 0)
                logits(NG - 1, 1)

                pe.wait_ge(s["mask_done"], m + 1)
                flat = MK[:, :, :].rearrange("p e t -> p (e t)")
                M.matmul(bank[6][:, 0:E * NT], tri_sb[:, :], flat, start=True, stop=True).then_inc(s["route_pe"], 1)
                M.matmul(bank[7][:, 0:E * NT], ones_sb[:, :], flat, start=True, stop=True).then_inc(s["route_pe"], 1)
                pe.wait_ge(s["experts_done"], m + 1)

                def turn_slots(i, q, k):
                    pe.wait_ge(s[f"xin{q}"], (m * (TILES // 4) + k + 1) * DMA)
                    wait(pe, s["slotT_act"], m * TILES + i)
                    M.transpose(bank[4][:, 0:P], xin[:, q, :], id_sb[:, :]).then_inc(s["slotT_pe"], 1)

                def gate(i, b, e):
                    pe.wait_ge(s["slotT_act"], m * TILES + i + 1)
                    wait(pe, s["silu_act"], m * TILES + i - 1)
                    M.matmul(bank[b][:, :], xT[:, b, :], wg_sb[:, bass.ds(e * I, I)],
                             start=True, stop=True).then_inc(s["gate_pe"], 1)

                def up(i, b, e):
                    wait(pe, s["hid_dve"], m * TILES + i - 1)
                    M.matmul(bank[2 + b][:, :], xT[:, b, :], wu_sb[:, bass.ds(e * I, I)],
                             start=True, stop=True).then_inc(s["up_pe"], 1)

                def turn_hidden(i, b):
                    pe.wait_ge(s["hid_dve"], m * TILES + i + 1)
                    wait(pe, s["hidT_act"], m * TILES + i)
                    for c in range(IC):
                        ins = M.transpose(bank[5][:, c * P:(c + 1) * P], hid[:, b, c * P:(c + 1) * P], id_sb[:, :])
                    ins.then_inc(s["hidT_pe"], 1)

                def down(i, b, e):
                    pe.wait_ge(s["hidT_act"], m * TILES + i + 1)
                    wait(pe, s["yo_act"], m * TILES + i)
                    for c in range(IC):
                        ins = M.matmul(bank[6][:, 0:D], hT[:, b, c * P:(c + 1) * P],
                                       wd_sb[:, bass.ds(e * IC + c, 1), :].rearrange("p c d -> p (c d)"),
                                       start=(c == 0), stop=(c == IC - 1))
                    ins.then_inc(s["down_pe"], 1)

                def expert_of(i):
                    return pe.value_load(te[0:1, bass.ds(i, 1)], min_val=0, max_val=E - 1)

                def tile(i, q, k, e_last):
                    if not (isinstance(i, int) and i == TILES - 1):
                        turn_slots(i + 1, (q + 1) % 4, k + 1 if q == 3 else k)
                    e = expert_of(i)
                    gate(i, q % 2, e)
                    if not (isinstance(i, int) and i == 0):
                        turn_hidden(i - 1, (q - 1) % 2)
                    up(i, q % 2, e)
                    if not (isinstance(i, int) and i == 0):
                        down(i - 1, (q - 1) % 2, e_last)
                    return e

                turn_slots(0, 0, 0)
                e = None
                for q in range(4):
                    e = tile(q, q, 0, e)
                with pe.Fori(1, TILES // 4 - 1) as k:
                    e = expert_of(k * 4 - 1)
                    for q in range(4):
                        e = tile(k * 4 + q, q, k, e)
                e = expert_of(TILES - 5)
                for q in range(4):
                    e = tile(TILES - 4 + q, q, TILES // 4 - 1, e)
                turn_hidden(TILES - 1, 1)
                down(TILES - 1, 1, e)

            moe(0)
            pe.wait_ge(s["yo_act"], TILES)

            def turn_norm(p):
                pe.wait_ge(s["dve_pre"], done(DVE_PRE, "xn", p))
                wait(pe, s["dve_post"], done(DVE_POST, "res", 2 * p - 2) if not isinstance(p, int) or p > 0 else 0)
                for t in range(G):
                    ins = M.transpose(bank[6][:, t * P:(t + 1) * P], xn4[:, t, :], id_sb[:, :])
                ins.then_inc(s["pe_pre"], 1)

            def project_in(p, r, part):
                if part == 0:
                    pe.wait_ge(s["act_pre"], done(ACT_PRE, "xnTrev", p))
                    if r == 1:
                        pe.wait_ge(s["act_pre"], done(ACT_PRE, "abs1_0", p))
                        wait(pe, s["dve_post"], done(DVE_POST, "res", 2 * p - 1) if not isinstance(p, int) or p > 0 else 0)
                else:
                    pe.wait_ge(s["dve_pre"], done(DVE_PRE, f"tap3c1_{r}", p))
                for c in range(C):
                    at = part * DI + c * P
                    M.matmul(bank[6 + c][:, :], in_sb[:, r, at:at + P],
                             xnT[:, r, :, :].rearrange("p s t -> p (s t)"),
                             start=True, stop=True).then_inc(s["pe_pre"], 1)

            def project_x(p, r):
                pe.wait_ge(s["act_pre"], done(ACT_PRE, f"xc{r}", p))
                for c in range(C):
                    ins = M.matmul(bank[6][0:2 * BC + RK, :], xp_sb[:, r, c, :], xc[r][:, c * W:(c + 1) * W],
                                   start=(c == 0), stop=(c == C - 1))
                ins.then_inc(s["pe_pre"], 1)

            def project_dt(p, r):
                pe.wait_ge(s["act_pre"], done(ACT_PRE, f"dts{r}", p))
                pe.wait_ge(s["dve_pre"], done(DVE_PRE, f"lo{r}", p))
                for c, bk in ((0, bank[7]), (1, bank[6])):
                    M.matmul(bk[:, :], dtp_sb[2 * BC:2 * BC + RK, r, c * P:(c + 1) * P],
                             dts[2 * BC:2 * BC + RK, :], start=True, stop=True).then_inc(s["pe_pre"], 1)

            def project_out(u, r, after):
                pe.wait_ge(s["dve_post"], done(DVE_POST, "gate", u))
                after()
                for t in range(G):
                    for c in range(C):
                        ins = M.matmul(bank[6][:, t * D:(t + 1) * D], gat[:, c * W + t * P:c * W + (t + 1) * P],
                                       out_sb[:, r, c, :], start=(c == 0), stop=(c == C - 1))
                ins.then_inc(s["pe_post"], 1)

            def spread_B(p, r, n):
                N = p * 2 * NS + r * NS + n
                wait(pe, s["mul_done"], N * 2)
                if n == 0:
                    pe.wait_ge(s["dve_pre"], done(DVE_PRE, f"lo{r}", p))
                M.matmul(bank[2][:, :], sel[:, n:n + 1].broadcast_to([2 * BC, P]), BCs[r][:, :],
                         start=True, stop=True).then_inc(s["bcB_ready"], 1)

            def spread_C(p, r, n):
                N = p * 2 * NS + r * NS + n
                wait(pe, s["Cs_ready"], N)
                M.matmul(bank[3][:, :], sel[:, NS + n:NS + n + 1].broadcast_to([2 * BC, P]), BCs[r][:, :],
                         start=True, stop=True).then_inc(s["bcC_ready"], 1)

            def sum_states(N, u, n, b):
                pe.wait_ge(s["hC_ready"], N + 1)
                if n == 0:
                    wait(pe, s["dve_post"], done(DVE_POST, "gate", u - 1) if not isinstance(u, int) or u > 0 else 0)
                for c in range(C):
                    ins = M.matmul(bank[4 + c][:, :], id_sb[:, :], hC[:, b, c * W:(c + 1) * W],
                                   start=(n == 0), stop=(n == NS - 1), skip_group_check=True)
                ins.then_inc(s["y_done"], 1)

            def pair(p, first, last):
                for r in range(2):
                    u = p * 2 + r
                    pv, rv = (p, 1) if r == 0 else (p + 1, 0)
                    prep = not (last and r == 1)
                    for n in range(NS):
                        N = p * 2 * NS + r * NS + n
                        spread_B(p, r, n)
                        spread_C(p, r, n)
                        if n > 0:
                            sum_states(N - 1, u, n - 1, (n - 1) % 2)
                        elif not (first and r == 0):
                            sum_states(N - 1, u - 1, NS - 1, (NS - 1) % 2)
                        if n == 1 and not (first and r == 0):
                            project_out(u - 1, 1 - r, lambda: pe.wait_ge(
                                s["act_pre"], done(ACT_PRE, f"abs1_{r}", p)))
                        if not prep:
                            continue
                        if n == 4 and rv == 0:
                            turn_norm(pv)
                        if n == 5:
                            project_in(pv, rv, 0)
                        if n == 10:
                            project_in(pv, rv, 1)
                        if n == 12:
                            project_x(pv, rv)
                        if n == 13:
                            project_dt(pv, rv)

            turn_norm(0)
            project_in(0, 0, 0)
            project_in(0, 0, 1)
            project_x(0, 0)
            project_dt(0, 0)
            pair(0, True, False)
            with pe.Fori(1, NP - 1) as p:
                pair(p, False, False)
            pair(NP - 1, False, True)
            sum_states(2 * NP * NS - 1, 2 * NP - 1, NS - 1, (NS - 1) % 2)
            project_out(2 * NP - 1, 1, lambda: pe.wait_ge(
                s["dve_post"], done(DVE_POST, "res", 2 * NP - 2)))
            pe.wait_ge(s["dve_post"], done(DVE_POST, "res", 2 * NP - 1))
            moe(1)


def kernel(**inputs):
    import numpy as np
    import concourse.bacc as bacc
    from concourse.bass_utils import run_bass_kernel_spmd

    a = {k.removeprefix("L0_"): np.asarray(v) for k, v in inputs.items()}
    x = a["attn_x"]
    T, D = x.shape[0] * x.shape[1], x.shape[2]
    wg, wu, wd = a["ffn_wg"], a["ffn_wu"], a["ffn_wd"]
    E, I, _ = wg.shape
    NT, IC = T // P, I // P
    NS, RK = a["attn_A_log1"].shape[1], a["attn_dtp_w1"].shape[1]
    DI = a["attn_A_log1"].shape[0]
    C = DI // P

    def chunks(v):
        return v.reshape(C, P, -1).transpose(1, 0, 2)

    def both(f):
        return np.ascontiguousarray(np.stack([f(1), f(2)]))

    def rows_bcbc_dt(w):
        return np.concatenate([w[RK:], w[RK:], w[:RK]], 0)

    tiles = -(-(-(-(2 * T + E * (P - 1)) // P)) // 4) * 4
    reset = np.ones((P, E, NT), np.float32)
    reset[:, :, 0] = 0.0
    arrays = {
        "x": x.reshape(T, D),
        "gateT": a["ffn_gate_w"].T,
        "wgT": wg.transpose(2, 0, 1).reshape(D, E * I),
        "wuT": wu.transpose(2, 0, 1).reshape(D, E * I),
        "wdT": wd.reshape(E, D, IC, P).transpose(3, 0, 2, 1).reshape(P, E * IC, D),
        "inT": both(lambda r: a[f"attn_in_w{r}"].T),
        "xpT": both(lambda r: chunks(rows_bcbc_dt(a[f"attn_xp_w{r}"]).T)),
        "dtpT": both(lambda r: a[f"attn_dtp_w{r}"].T),
        "chan": both(lambda r: chunks(np.concatenate(
            [a[f"attn_conv_w{r}"].reshape(DI, -1), a[f"attn_conv_b{r}"].reshape(DI, 1),
             a[f"attn_dtp_b{r}"].reshape(DI, 1), a[f"attn_Dvec{r}"].reshape(DI, 1),
             a[f"attn_A_log{r}"]], 1))),
        "outT": both(lambda r: chunks(a[f"attn_out_w{r}"].T)),
        "ident": np.eye(P, dtype=np.float32),
        "tri": np.triu(np.ones((P, P), np.float32), 1),
        "e_rank": np.tile(np.arange(E, 0, -1, dtype=np.float32), (P, 1)),
        "e_reset": reset.reshape(P, E * NT),
        "tile_rank": np.arange(tiles, dtype=np.float32).reshape(1, tiles),
    }
    nc = bacc.Bacc("TRN2", target_bir_lowering=False, num_devices=1)
    launch, args = {}, []
    for name, v in arrays.items():
        v = np.ascontiguousarray(v)
        launch[name] = v
        args.append(nc.dram_tensor(name, v.shape, mybir.dt.from_np(v.dtype), kind="ExternalInput").ap())
    out = nc.dram_tensor("out", (T, D), F32, kind="ExternalOutput").ap()
    macaron_kernel(nc, *args, out)
    r = run_bass_kernel_spmd(nc, [launch], core_ids=[0])
    return r.results[0]["out"].reshape(x.shape)
```

```python
from contextlib import ExitStack

import concourse.bass as bass
from concourse import mybir

F32 = mybir.dt.float32
F32R = mybir.dt.float32r
I32 = mybir.dt.int32
U32 = mybir.dt.uint32
ALU = mybir.AluOpType
ACT = mybir.ActivationFunctionType
AX_X = mybir.AxisListType.X
P = 128
DMA = 16
EPS = 1e-5

DVE_PRE = [f"{s}{r}" for r in (0, 1) for s in (
    "tap1c0_", "tap1c1_", "tap2c0_", "tap2c1_", "tap3c0_", "tap3c1_", "lo", "delta", "du")]
ACT_PRE = [f"{s}{r}" for r in (0, 1) for s in (
    "conv0_", "conv1_", "zs0_", "zs1_", "xc", "hi", "dts", "relu0_", "abs0_", "relu1_", "abs1_",
    "exp", "ln")]
PE_PRE = [f"{s}{r}" for r in (0, 1) for s in (
    "xi0_", "xi1_", "z0_", "z1_", "xdbl", "dt0_", "dt1_")]
DVE_NORM = ["stats", "aggr", "vareps", "xn"]
ACT_NORM = ["xnT", "xnTrev"]
DVE_AT = {"taps": (1, 2, 3), "skip": 2, "gate": 4, "lo": 8, "size": 12, "res": 12, "stats": 6, "xn": 10}
POOL_RSTD = 8
DECAY_LEAD, COPY_LEAD, SPREAD_LEAD, SUM_LAG = 3, 1, 2, 2
ACT_AT = {"conv": 0, "silus": 6, "hi": 8, "parts": 10, "ln": 11, "xnT": 14}
PE_AT = {"xi": 0, "z": 5, "xdbl": 7, "dt": 9, "out": 11, "xt": 13}
DVE_POST = ["skip0", "skip1", "gate", "res"]


def done(steps, name, turn):
    return turn * len(steps) + steps.index(name) + 1


def wait(eng, sem, value):
    if isinstance(value, int) and value <= 0:
        return
    eng.wait_ge(sem, value)


def macaron_kernel(nc, x, gateT, wgT, wuT, wdT, inT, xpT, dtpT, chan, outT, ident, tri, e_rank,
                   e_reset, tile_rank, out):
    T, D = x.shape
    L = 256
    NT = T // P
    NP = T // (2 * L)
    E = gateT.shape[1]
    I = wgT.shape[1] // E
    IC = I // P
    DI = inT.shape[2] // 2
    C = DI // P
    NS = 16
    RK = dtpT.shape[1]
    BC = 2 * NS
    S = 2
    W = S * L
    G = 4
    NG = NT // G
    TILES = -(-(2 * T + E * (P - 1)) // P)
    TILES = -(-TILES // 4) * 4
    assert D == P and C == 2 and I == 512 and W == 512 and NG == NP and NG % 2 == 0
    CONV, CB, DTB, DSK, ALOG = 0, 4, 5, 6, 7

    xs = nc.dram_tensor("slot_rows", [TILES * P, D], F32, kind="Internal").ap()
    ys = nc.dram_tensor("slot_outputs", [TILES * P, D], F32, kind="Internal").ap()

    with ExitStack() as ctx:
        def sb(name, shape, dt=F32):
            return ctx.enter_context(nc.sbuf_tensor(name, shape, dt))

        def sem(name):
            return ctx.enter_context(nc.semaphore(name))

        X = sb("X", [P, NT, D])
        wgu = sb("wgu", [P, 2 * E * I])
        wg_sb, wu_sb = wgu[:, 0:E * I], wgu[:, E * I:2 * E * I]
        wd_sb = sb("wd_sb", [P, E * IC, D])
        gate_sb = sb("gate_sb", [P, E])
        in_sb = sb("in_sb", [P, 2, 2 * DI])
        xp_sb = sb("xp_sb", [P, 2, C, 2 * BC + RK])
        dtp_sb = sb("dtp_sb", [2 * BC + RK, 2, DI])
        out_sb = sb("out_sb", [P, 2, C, D])
        ch = sb("ch", [P, 2, C, ALOG + NS])
        negA = sb("negA", [P, 2, C, NS])
        id_sb = sb("id_sb", [P, P])
        tri_sb = sb("tri_sb", [P, P])
        ones_sb = sb("ones_sb", [P, P])
        half = sb("half", [P, NT])
        sel = sb("sel", [2 * BC, BC], F32R)
        assert 8 * C * W <= 2 * E * I
        unit = [wgu[:, k * C * W:(k + 1) * C * W] for k in range(8)]
        MV = sb("MV", [P, G, 2])
        st = sb("st", [P, G, 6])
        ve = sb("ve", [P, NT])
        rs = sb("rs", [P, NT])
        mean = sb("mean", [P, NT])
        best = sb("best", [P, 2, NT])
        wt = sb("wt", [P, 2, NT])
        rank_sb = sb("rank_sb", [P, E])
        er_sb = sb("er_sb", [P, E * NT])
        tn_sb = sb("tn_sb", [1, TILES])
        I1 = sb("I1", [P, 2, NT])
        cnt = sb("cnt", [P, 4, E])
        cnti = sb("cnti", [P, 2, E], I32)
        SLf = sb("SLf", [P, 2, NT])
        SL = sb("SL", [P, NT, 2], U32)
        tef = sb("tef", [1, TILES])
        te = sb("te", [1, TILES], I32)
        R = 4
        BUF = R * (4 * C * W + W) + 4 * C * W
        buf = sb("buf", [P, BUF])

        def carve(at, n):
            return buf[:, at:at + n]

        xin = carve(0, 4 * D).rearrange("p (b d) -> p b d", d=D)
        xT = carve(512, 4 * P).rearrange("p (b d) -> p b d", d=P)
        sg = carve(1024, 2 * I).rearrange("p (b d) -> p b d", d=I)
        hid = carve(2048, 2 * I).rearrange("p (b d) -> p b d", d=I)
        hT = carve(3072, 2 * I).rearrange("p (b d) -> p b d", d=I)
        yo = carve(4096, 4 * D).rearrange("p (b d) -> p b d", d=D)
        rowsA = carve(4608, 2 * G * D).rearrange("p (b t d) -> p b t d", t=G, d=D)
        rowsB = carve(5632, 2 * G * D).rearrange("p (b t d) -> p b t d", t=G, d=D)
        xnTr = carve(6656, 2 * G * P).rearrange("p (b d) -> p b d", d=G * P)
        ZERO = 2048
        zero = carve(4608, ZERO)
        ZEROED = -(-TILES // (ZERO // D)) * DMA
        idx = sb("idx", [P, 2, 2 * G], U32)

        rowsN = carve(7680, 2 * G * D).rearrange("p (b t d) -> p b t d", t=G, d=D)
        LG = carve(8704, NT * E).rearrange("p (t e) -> p t e", e=E)
        O12 = carve(9216, 2 * E * NT).rearrange("p (k e t) -> p k e t", k=2, e=E)
        MK = carve(10240, E * NT).rearrange("p (e t) -> p e t", e=E)
        CS = carve(10752, E * NT)
        ST = carve(11264, NT * 6).rearrange("p (t k) -> p t k", k=6)
        tc8 = buf[0:1, 11648:11648 + TILES * E].rearrange("p (t e) -> p t e", e=E)
        assert 11648 + TILES * E <= BUF

        CW = C * W
        dA = carve(0, R * CW).rearrange("p (b c s t) -> p b c s t", b=R, c=C, s=S)
        prod = carve(R * CW, R * CW).rearrange("p (b w) -> p b w", b=R)
        hs = carve(2 * R * CW, R * CW).rearrange("p (b w) -> p b w", b=R)
        hC = carve(3 * R * CW, R * CW).rearrange("p (b w) -> p b w", b=R)
        Cs = carve(4 * R * CW, R * W).rearrange("p (b w) -> p b w", b=R)
        rest = R * (4 * CW + W)
        tmp = carve(rest, CW)
        xnT = carve(rest + CW, 2 * W).rearrange("p (b s t) -> p b s t", b=2, s=S)
        gat = carve(rest + 2 * CW, CW)
        xn4 = carve(rest + 3 * CW, W).rearrange("p (t d) -> p t d", d=D)
        dts = carve(rest + 3 * CW + W, W)
        BCs = [sb(f"BCs{r}", [2 * BC, W], F32R) for r in (0, 1)]
        xc = [unit[0], unit[4]]
        zs = [unit[1], unit[5]]
        delta = [unit[2], unit[6]]
        du = [unit[3], unit[7]]

        bank = [ctx.enter_context(nc.psum_tensor(f"bank{i}", [P, 512], F32)) for i in range(8)]

        names = """scatter_turn gather_turn aggr_turn loaded_x loaded_w zeroed consts stats_done dve_norm act_norm xt_pre vareps_done rstd_done xn_done
            xt_done xnT_done logit_done logits_act route_dve route_pe route_act stage_done scat0 scat1
            xin0 xin1 xin2 xin3 st0 st1 st2 st3 slotT_pe slotT_act gate_pe up_pe silu_act hid_dve
            hidT_pe hidT_act down_pe yo_act gath0 gath1 comb_done comb_first idx_done stored diff_done mask_done slots_done experts_done expA_done
            dve_pre act_pre pe_pre rstd_pre dve_post pe_post negA_done
            bcB_ready bcC_ready dA_ready mul_done scan_done Cs_ready hC_ready y_done""".split()
        s = {n: sem(n) for n in names}
        block = ctx.enter_context(nc.Block())

        NITER = NG // 2
        @block.sync
        def _(sp):
            sp.dma_start(X[:, :, :], x.rearrange("(t p) d -> p t d", p=P)).then_inc(s["loaded_x"], DMA)
            small = [(id_sb[:, :], ident), (tri_sb[:, :], tri), (gate_sb[:, :], gateT),
                     (rank_sb[:, :], e_rank), (er_sb[:, :], e_reset), (tn_sb[:, :], tile_rank),
                     (in_sb[:, :, :], inT.rearrange("r p n -> p r n")),
                     (xp_sb[:, :, :, :], xpT.rearrange("r p c n -> p r c n")),
                     (dtp_sb[2 * BC:, :, :], dtpT.rearrange("r k n -> k r n")),
                     (ch[:, :, :, :], chan.rearrange("r p c n -> p r c n")),
                     (out_sb[:, :, :, :], outT.rearrange("r p c n -> p r c n")),
                     (wg_sb, wgT), (wu_sb, wuT), (wd_sb[:, :, :], wdT)]
            for dst, src in small:
                sp.dma_start(dst, src).then_inc(s["loaded_w"], DMA)

            def load_slots(m, i, b):
                wait(sp, s["slotT_pe"], m * TILES + i - 3)
                sp.dma_start(xin[:, b, :], xs[bass.ds(i * P, P), :]).then_inc(s[f"xin{b}"], DMA)

            def experts(m):
                sp.wait_ge(s["scat0"], (m + 1) * NG // 2 * 2 * G * DMA)
                sp.wait_ge(s["scat1"], (m + 1) * NG // 2 * 2 * G * DMA)
                for i in range(4):
                    load_slots(m, i, i)

                def store(i, b):
                    sp.wait_ge(s["yo_act"], m * TILES + i + 1)
                    sp.dma_start(ys[bass.ds(i * P, P), :], yo[:, b, :]).then_inc(s[f"st{b}"], DMA)

                with sp.Fori(0, TILES // 4 - 1) as k:
                    for b in range(4):
                        load_slots(m, k * 4 + 4 + b, b)
                        store(k * 4 + b, b)
                for b in range(4):
                    store(TILES - 4 + b, b)

            experts(0)
            sp.wait_ge(s["dve_post"], done(DVE_POST, "gate", 2 * NP - 1))
            sp.dma_start(wg_sb, wgT).then_inc(s["loaded_w"], DMA)
            sp.dma_start(wu_sb, wuT).then_inc(s["loaded_w"], DMA)
            experts(1)
            for g in range(NG):
                sp.wait_ge(s["comb_done"], NG + g + 1)
                sp.dma_start(out[g * G * P:(g + 1) * G * P, :].rearrange("(t p) d -> p t d", p=P),
                             X[:, g * G:(g + 1) * G, :]).then_inc(s["stored"], DMA)
            sp.wait_ge(s["stored"], NG * DMA)

        @block.gpsimd
        def _(pool):
            pool.memset(ones_sb[:, :], 1.0).then_inc(s["consts"], 1)
            pool.memset(half[:, :], -0.5).then_inc(s["consts"], 1)
            pool.memset(zero, 0.0).then_inc(s["consts"], 1)
            pool.wait_ge(s["consts"], 3)
            ZT = ZERO // D
            for a in range(0, TILES, ZT):
                n = min(ZT, TILES - a)
                pool.dma_start(xs[a * P:(a + n) * P, :].rearrange("(t p) d -> p t d", p=P),
                               zero[:, 0:n * D].rearrange("p (t d) -> p t d", d=D)).then_inc(s["zeroed"], DMA)

            def moe(m):
                if m == 0:
                    pool.wait_ge(s["zeroed"], ZEROED)
                pool.wait_ge(s["vareps_done"], m + 1)
                pool.tensor_tensor(rs[:, :], ve[:, :], half[:, :], ALU.pow).then_inc(s["rstd_done"], 1)

                def scatter(g, b):
                    pool.wait_ge(s["stage_done"], m * NG + g + 1)
                    pool.sem_inc(s["scatter_turn"], 1)
                    for t in range(G):
                        for k in range(2):
                            pool.indirect_dma_start(
                                out=xs[:, :], out_offset=bass.IndirectOffsetOnAxis(
                                    ap=idx[:, b, 2 * t + k:2 * t + k + 1], axis=0),
                                in_=rowsA[:, b, t, :], in_offset=None).then_inc(s[f"scat{b}"], DMA)

                with pool.Fori(0, NITER) as i:
                    for b in range(2):
                        scatter(i * 2 + b, b)

                for b in range(4):
                    pool.wait_ge(s[f"st{b}"], (m + 1) * TILES // 4 * DMA)

                def gather(g, b):
                    pool.wait_ge(s["idx_done"], m * NG + g + 1)
                    wait(pool, s["comb_done"], m * NG + g - 1)
                    pool.sem_inc(s["gather_turn"], 1)
                    for t in range(G):
                        for k, rows in ((0, rowsA), (1, rowsB)):
                            pool.indirect_dma_start(
                                out=rows[:, b, t, :], out_offset=None, in_=ys[:, :],
                                in_offset=bass.IndirectOffsetOnAxis(
                                    ap=idx[:, b, 2 * t + k:2 * t + k + 1], axis=0)).then_inc(s[f"gath{b}"], DMA)

                for b in range(2):
                    gather(b, b)
                with pool.Fori(1, NITER) as i:
                    for b in range(2):
                        gather(i * 2 + b, b)

            moe(0)

            def rstd(p):
                pool.wait_ge(s["dve_norm"], done(DVE_NORM, "vareps", p))
                pool.tensor_tensor(rs[:, 0:G], ve[:, 0:G], half[:, 0:G], ALU.pow).then_inc(s["rstd_pre"], 1)

            def pair(p, first, last):
                for r in range(2):
                    for n in range(NS):
                        N = p * 2 * NS + r * NS + n
                        b = n % R
                        pool.wait_ge(s["scan_done"], N + 1)
                        pool.wait_ge(s["Cs_ready"], N + 1)
                        wait(pool, s["y_done"], N + 1 - R)
                        pool.tensor_tensor(hC[:, b, :].rearrange("p (c w) -> p c w", c=C),
                                           hs[:, b, :].rearrange("p (c w) -> p c w", c=C),
                                           Cs[:, b, :].unsqueeze(1).broadcast_to([P, C, W]),
                                           ALU.mult).then_inc(s["hC_ready"], 1)
                        if r == 0 and n == POOL_RSTD and not last:
                            rstd(p + 1)

            rstd(0)
            pair(0, True, False)
            with pool.Fori(1, NP - 1) as p:
                pair(p, False, False)
            pair(NP - 1, False, True)
            moe(1)

        @block.vector
        def _(dve):
            V = nc.vector
            seq = [0]

            def chain(ins, name="route_dve", count=0):
                if name == "route_dve":
                    seq[0] += 1
                    count = seq[0]
                ins.then_inc(s[name], 1)
                dve.wait_ge(s[name], count)

            dve.wait_ge(s["loaded_w"], 14 * DMA)
            dve.wait_ge(s["loaded_x"], DMA)
            dve.wait_ge(s["consts"], 3)
            V.tensor_copy(sel[0:BC, :], id_sb[0:BC, 0:BC])
            chain(V.tensor_copy(sel[BC:2 * BC, :], id_sb[BC:2 * BC, BC:2 * BC]))

            def moe(m):
                def stats(g):
                    for t in range(G):
                        ins = V.bn_stats(ST[:, bass.ds(g * G + t, 1), :], X[:, bass.ds(g * G + t, 1), :])
                    ins.then_inc(s["stats_done"], 1)

                with dve.Fori(0, NG) as g:
                    stats(g)
                dve.wait_ge(s["stats_done"], (m + 1) * NG)
                chain(V.tensor_tensor(mean[:, :], ST[:, :, 1], ST[:, :, 4], ALU.add))
                chain(V.tensor_tensor(ve[:, :], ST[:, :, 1], ST[:, :, 4], ALU.subtract))
                chain(V.tensor_scalar(mean[:, :], mean[:, :], 0.5, None, ALU.mult))
                chain(V.scalar_tensor_tensor(out=ve[:, :], in0=ve[:, :], scalar=0.25, in1=ve[:, :],
                                             op0=ALU.mult, op1=ALU.mult))
                chain(V.tensor_tensor(rs[:, :], ST[:, :, 2], ST[:, :, 5], ALU.add))
                chain(V.scalar_tensor_tensor(out=ve[:, :], in0=rs[:, :], scalar=1.0 / D, in1=ve[:, :],
                                             op0=ALU.mult, op1=ALU.add))
                V.tensor_scalar(ve[:, :], ve[:, :], EPS, None, ALU.add).then_inc(s["vareps_done"], 1)
                dve.wait_ge(s["rstd_done"], m + 1)

                def normalise(g, rows):
                    for t in range(G):
                        ins = V.tensor_scalar(rows[:, t:t + 1, :], X[:, bass.ds(g * G + t, 1), :],
                                              mean[:, bass.ds(g * G + t, 1)], rs[:, bass.ds(g * G + t, 1)],
                                              ALU.subtract, ALU.mult)
                    return ins

                def normalise_for_logits(g, b):
                    wait(dve, s["xt_done"], m * NG + g - 1)
                    normalise(g, rowsN[:, b, :, :]).then_inc(s["xn_done"], 1)

                for b in range(2):
                    normalise_for_logits(b, b)
                with dve.Fori(1, NITER) as i:
                    for b in range(2):
                        normalise_for_logits(i * 2 + b, b)
                dve.wait_ge(s["logits_act"], (m + 1) * NG)

                LGe = LG[:, :, :].rearrange("p t e -> p e t")
                for k in range(2):
                    one = O12[:, k, :, :]
                    chain(V.tensor_reduce(best[:, k, :], LG[:, :, :], AX_X, ALU.max))
                    chain(V.tensor_tensor(one, LGe, best[:, k, :].unsqueeze(1).broadcast_to([P, E, NT]),
                                          ALU.is_equal))
                    chain(V.tensor_tensor(one, one, rank_sb[:, :].unsqueeze(2).broadcast_to([P, E, NT]), ALU.mult))
                    chain(V.tensor_reduce(I1[:, k, :], one.rearrange("p e t -> p t e"), AX_X, ALU.max))
                    chain(V.tensor_tensor(one, rank_sb[:, :].unsqueeze(2).broadcast_to([P, E, NT]),
                                          I1[:, k, :].unsqueeze(1).broadcast_to([P, E, NT]), ALU.is_equal))
                    if k == 0:
                        chain(V.scalar_tensor_tensor(out=LG[:, :, :], in0=one.rearrange("p e t -> p t e"),
                                                     scalar=-3e38, in1=LG[:, :, :], op0=ALU.mult, op1=ALU.add))
                chain(V.tensor_tensor(MK[:, :, :], O12[:, 0, :, :], O12[:, 1, :, :], ALU.add), "mask_done", m + 1)

                chain(V.tensor_tensor(SLf[:, 0, :], best[:, 1, :], best[:, 0, :], ALU.subtract), "diff_done", m + 1)
                dve.wait_ge(s["route_act"], m + 1)
                chain(V.tensor_scalar(SLf[:, 0, :], SLf[:, 1, :], 1.0, None, ALU.add))
                chain(V.reciprocal(SLf[:, 0, :], SLf[:, 0, :]))
                chain(V.tensor_scalar(wt[:, 0, :], SLf[:, 0, :], 0.5, None, ALU.mult))
                chain(V.tensor_tensor(wt[:, 1, :], wt[:, 0, :], SLf[:, 1, :], ALU.mult))
                dve.wait_ge(s["route_pe"], 2 * m + 2)
                tot = bank[7][:, 0:E * NT]
                chain(V.tensor_tensor_scan(CS[:, :], er_sb[:, :], tot, 0.0, ALU.mult, ALU.add))
                CS3 = CS[:, :].rearrange("p (e t) -> p e t", e=E)
                chain(V.tensor_scalar(cnti[:, 0, :], CS3[:, :, NT - 1], float(P - 1), None, ALU.add))
                chain(V.tensor_scalar(cnti[:, 1, :], cnti[:, 0, :], 7, None, ALU.logical_shift_right))
                chain(V.tensor_copy(cnt[:, 0, :], cnti[:, 1, :]))
                chain(V.tensor_tensor_scan(cnt[:, 1, :], ones_sb[:, 0:E], cnt[:, 0, :], 0.0, ALU.mult, ALU.add))
                chain(V.tensor_tensor(cnt[:, 2, :], cnt[:, 1, :], cnt[:, 0, :], ALU.subtract))
                chain(V.tensor_scalar(cnt[:, 3, :], cnt[:, 2, :], float(P), None, ALU.mult))
                chain(V.tensor_tensor(CS[:, :], CS[:, :], tot, ALU.subtract))
                chain(V.tensor_tensor(CS[:, :], CS[:, :], bank[6][:, 0:E * NT], ALU.add))
                chain(V.tensor_tensor(CS3, CS3, cnt[:, 3, :].unsqueeze(2).broadcast_to([P, E, NT]), ALU.add))
                for k in range(2):
                    chain(V.tensor_tensor(O12[:, k, :, :], O12[:, k, :, :], CS3, ALU.mult))
                    chain(V.tensor_reduce(SLf[:, k, :], O12[:, k, :, :].rearrange("p e t -> p t e"), AX_X, ALU.add))
                chain(V.tensor_copy(SL[:, :, :], SLf[:, :, :].rearrange("p k t -> p t k")), "slots_done", m + 1)
                chain(V.tensor_tensor(tc8[:, :, :], tn_sb[:, :].unsqueeze(2).broadcast_to([1, TILES, E]),
                                      cnt[0:1, 1, :].unsqueeze(1).broadcast_to([1, TILES, E]), ALU.is_ge))
                chain(V.tensor_reduce(tef[:, :], tc8[:, :, :], AX_X, ALU.add))
                chain(V.tensor_scalar(te[:, :], tef[:, :], float(E - 1), None, ALU.min), "experts_done", m + 1)

                dve.wait_ge(s["zeroed"], ZEROED)

                def stage(g, b, k):
                    wait(dve, s[f"scat{b}"], (m * NITER + k) * 2 * G * DMA)
                    normalise(g, rowsA[:, b, :, :])
                    V.tensor_copy(idx[:, b, :], SL[:, bass.ds(g * G, G), :].rearrange("p t k -> p (t k)")
                                  ).then_inc(s["stage_done"], 1)

                for b in range(2):
                    stage(b, b, 0)
                with dve.Fori(1, NITER) as i:
                    for b in range(2):
                        stage(i * 2 + b, b, i)

                def hidden(i, b):
                    dve.wait_ge(s["silu_act"], m * TILES + i + 1)
                    dve.wait_ge(s["up_pe"], m * TILES + i + 1)
                    wait(dve, s["hidT_pe"], m * TILES + i - 1)
                    V.tensor_tensor(hid[:, b, :], sg[:, b, :], bank[2 + b][:, :], ALU.mult).then_inc(s["hid_dve"], 1)

                hidden(0, 0)
                hidden(1, 1)
                with dve.Fori(1, TILES // 2) as k:
                    for b in range(2):
                        hidden(k * 2 + b, b)

                def combine(g, b, k):
                    dve.wait_ge(s[f"gath{b}"], (m * NITER + k + 1) * 2 * G * DMA)
                    for w, rows in ((0, rowsA), (1, rowsB)):
                        for t in range(G):
                            xt = X[:, bass.ds(g * G + t, 1), :]
                            ins = V.scalar_tensor_tensor(out=xt, in0=rows[:, b, t:t + 1, :],
                                                         scalar=wt[:, w, bass.ds(g * G + t, 1)],
                                                         in1=xt, op0=ALU.mult, op1=ALU.add)
                        if w == 0:
                            ins.then_inc(s["comb_first"], 1)
                            dve.wait_ge(s["comb_first"], m * NG + g + 1)
                    ins.then_inc(s["comb_done"], 1)

                with dve.Fori(0, NITER) as i:
                    for b in range(2):
                        combine(i * 2 + b, b, i)
                dve.wait_ge(s["comb_done"], (m + 1) * NG)

            moe(0)

            dve.wait_ge(s["expA_done"], 1)
            V.tensor_scalar(negA[:, :, :, :], negA[:, :, :, :], -1.0, None, ALU.mult).then_inc(s["negA_done"], 1)
            dve.wait_ge(s["yo_act"], TILES)
            chain(V.memset(dA[:, :, :, :, 0:1], 0.0))

            def step_done(name, turn):
                dve.wait_ge(s["dve_pre"], done(DVE_PRE, name, turn))

            def layernorm(p):
                wait(dve, s["dve_norm"], done(DVE_NORM, "xn", p - 1))
                for t in range(G):
                    ins = V.bn_stats(st[:, t, :], X[:, bass.ds(p * G + t, 1), :])
                ins.then_inc(s["dve_norm"], 1)
                dve.wait_ge(s["dve_norm"], done(DVE_NORM, "stats", p))
                dve.sem_inc(s["aggr_turn"], 1)
                for t in range(G):
                    ins = V.bn_aggr(MV[:, t, :], st[:, t, :])
                ins.then_inc(s["dve_norm"], 1)
                dve.wait_ge(s["dve_norm"], done(DVE_NORM, "aggr", p))
                V.tensor_scalar(ve[:, 0:G], MV[:, :, 1], EPS, None, ALU.add).then_inc(s["dve_norm"], 1)

            def normalise(p):
                dve.wait_ge(s["rstd_pre"], p + 1)
                wait(dve, s["xt_pre"], p)
                for t in range(G):
                    ins = V.tensor_scalar(xn4[:, t, :], X[:, bass.ds(p * G + t, 1), :], MV[:, t, 0:1],
                                          rs[:, t:t + 1], ALU.subtract, ALU.mult)
                ins.then_inc(s["dve_norm"], 1)

            def taps(p, r, j):
                for c in range(C):
                    acc = tmp.rearrange("p (c s t) -> p c s t", c=C, s=S)[:, c, :, j:]
                    xi = bank[6 + c][:, :].rearrange("p (s t) -> p s t", s=S)[:, :, 0:L - j]
                    if j == 1:
                        dve.wait_ge(s["act_pre"], done(ACT_PRE, f"conv1_{r}", p))
                    else:
                        step_done(f"tap{j - 1}c{c}_{r}", p)
                    V.scalar_tensor_tensor(out=acc, in0=xi, scalar=ch[:, r, c, 3 - j:4 - j], in1=acc,
                                           op0=ALU.mult, op1=ALU.add).then_inc(s["dve_pre"], 1)

            def split_lo(p, r):
                dve.wait_ge(s["act_pre"], done(ACT_PRE, f"dts{r}", p))
                V.tensor_tensor(BCs[r][BC:2 * BC, :], bank[6][BC:2 * BC, :], BCs[r][BC:2 * BC, :].bitcast(F32),
                                ALU.subtract).then_inc(s["dve_pre"], 1)

            def step_size(p, r):
                dve.wait_ge(s["act_pre"], done(ACT_PRE, f"ln{r}", p))
                V.tensor_tensor(delta[r], delta[r], tmp, ALU.add).then_inc(s["dve_pre"], 1)
                step_done(f"delta{r}", p)
                V.tensor_tensor(du[r], delta[r], xc[r], ALU.mult).then_inc(s["dve_pre"], 1)

            def post_skip(u, r):
                dve.wait_ge(s["y_done"], (u + 1) * NS)
                wait(dve, s["pe_post"], u)
                for c in range(C):
                    V.scalar_tensor_tensor(out=gat[:, c * W:(c + 1) * W], in0=xc[r][:, c * W:(c + 1) * W],
                                           scalar=ch[:, r, c, DSK:DSK + 1], in1=bank[4 + c][:, :],
                                           op0=ALU.mult, op1=ALU.add).then_inc(s["dve_post"], 1)

            def post_gate(u, r):
                dve.wait_ge(s["dve_post"], done(DVE_POST, "skip1", u))
                V.tensor_tensor(gat, gat, zs[r], ALU.mult).then_inc(s["dve_post"], 1)

            def post_residual(u, p, r):
                dve.wait_ge(s["pe_post"], u + 1)
                xp4 = X[:, bass.ds(p * G, G), :]
                V.tensor_tensor(xp4, xp4, bank[6][:, :].rearrange("p (t d) -> p t d", t=G),
                                ALU.add).then_inc(s["dve_post"], 1)

            def product(p, r, n):
                N = p * 2 * NS + r * NS + n
                if n == 0:
                    dve.wait_ge(s["dve_pre"], done(DVE_PRE, f"du{r}", p))
                dve.wait_ge(s["bcB_ready"], N + 1)
                wait(dve, s["scan_done"], N + 1 - R)
                V.tensor_tensor(prod[:, n % R, :].rearrange("p (c w) -> p c w", c=C),
                                du[r].rearrange("p (c w) -> p c w", c=C),
                                bank[n % 2][:, :].unsqueeze(1).broadcast_to([P, C, W]),
                                ALU.mult).then_inc(s["mul_done"], 1)

            def scan(p, r, n):
                N = p * 2 * NS + r * NS + n
                b = n % R
                dve.wait_ge(s["dA_ready"], N + 1)
                wait(dve, s["hC_ready"], N + 1 - R)
                dve.wait_ge(s["mul_done"], N + 1)
                V.tensor_tensor_scan(hs[:, b, :], dA[:, b, :, :, :].rearrange("p c s t -> p (c s t)"),
                                     prod[:, b, :], 0.0, ALU.mult, ALU.add).then_inc(s["scan_done"], 1)

            def pair(p, first, last):
                for r in range(2):
                    u = p * 2 + r
                    pv, rv = (p, 1) if r == 0 else (p + 1, 0)
                    prep = not (last and r == 1)
                    for n in range(NS):
                        if n < NS - 1:
                            product(p, r, n + 1)
                        elif prep:
                            product(pv, rv, 0)
                        scan(p, r, n)
                        if not (first and r == 0):
                            if n == DVE_AT["skip"]:
                                post_skip(u - 1, 1 - r)
                            if n == DVE_AT["gate"]:
                                post_gate(u - 1, 1 - r)
                            if n == DVE_AT["res"]:
                                post_residual(u - 1, p - 1 if r == 0 else p, 1 - r)
                        if not prep:
                            continue
                        if n in DVE_AT["taps"]:
                            taps(pv, rv, n - DVE_AT["taps"][0] + 1)
                        if n == DVE_AT["lo"]:
                            split_lo(pv, rv)
                        if n == DVE_AT["size"]:
                            step_size(pv, rv)
                        if r == 0 and not last:
                            if n == DVE_AT["stats"]:
                                layernorm(p + 1)
                            if n == DVE_AT["xn"]:
                                normalise(p + 1)

            layernorm(0)
            normalise(0)
            for j in (1, 2, 3):
                taps(0, 0, j)
            split_lo(0, 0)
            step_size(0, 0)
            product(0, 0, 0)
            pair(0, True, False)
            with dve.Fori(1, NP - 1) as p:
                pair(p, False, False)
            pair(NP - 1, False, True)
            post_skip(2 * NP - 1, 1)
            post_gate(2 * NP - 1, 1)
            post_residual(2 * NP - 1, NP - 1, 1)
            dve.wait_ge(s["dve_post"], done(DVE_POST, "res", 2 * NP - 1))
            moe(1)

        @block.scalar
        def _(act):
            A = nc.scalar
            act.wait_ge(s["loaded_w"], 14 * DMA)
            A.activation(negA[:, :, :, :], ch[:, :, :, ALOG:ALOG + NS], ACT.Exp).then_inc(s["expA_done"], 1)

            def moe(m):
                def evacuate(g, b):
                    act.wait_ge(s["xt_done"], m * NG + g + 1)
                    wait(act, s["logit_done"], m * NG + g - 1)
                    A.activation(xnTr[:, b, :], bank[b][:, :], ACT.Copy).then_inc(s["xnT_done"], 1)

                def copy_logits(g, b):
                    act.wait_ge(s["logit_done"], m * NG + g + 1)
                    A.activation(LG[:, bass.ds(g * G, G), :], bank[4 + b][:, 0:G * E].rearrange("p (t e) -> p t e", e=E),
                                 ACT.Copy).then_inc(s["logits_act"], 1)

                evacuate(0, 0)
                for b in range(2):
                    evacuate(b + 1, 1 - b)
                    copy_logits(b, b)
                with act.Fori(1, NITER - 1) as i:
                    for b in range(2):
                        evacuate(i * 2 + b + 1, 1 - b)
                        copy_logits(i * 2 + b, b)
                evacuate(NG - 1, 1)
                copy_logits(NG - 2, 0)
                copy_logits(NG - 1, 1)
                act.wait_ge(s["diff_done"], m + 1)
                A.activation(SLf[:, 1, :], SLf[:, 0, :], ACT.Exp).then_inc(s["route_act"], 1)

                def copy_slotT(i, b):
                    act.wait_ge(s["slotT_pe"], m * TILES + i + 1)
                    wait(act, s["up_pe"], m * TILES + i - 1)
                    A.activation(xT[:, b, :], bank[4][:, 0:P], ACT.Copy).then_inc(s["slotT_act"], 1)

                def silu(i, b):
                    act.wait_ge(s["gate_pe"], m * TILES + i + 1)
                    wait(act, s["hid_dve"], m * TILES + i - 1)
                    A.activation(sg[:, b, :], bank[b][:, :], ACT.Silu).then_inc(s["silu_act"], 1)

                def copy_hidT(i, b):
                    act.wait_ge(s["hidT_pe"], m * TILES + i + 1)
                    wait(act, s["down_pe"], m * TILES + i - 1)
                    A.activation(hT[:, b, :], bank[5][:, :], ACT.Copy).then_inc(s["hidT_act"], 1)

                def copy_out(i, b2, k):
                    act.wait_ge(s["down_pe"], m * TILES + i + 1)
                    wait(act, s[f"st{b2}"], (m * (TILES // 4) + k) * DMA)
                    A.activation(yo[:, b2, :], bank[6][:, 0:D], ACT.Copy).then_inc(s["yo_act"], 1)

                def tile(i, q, k):
                    if not (isinstance(i, int) and i == TILES - 1):
                        copy_slotT(i + 1, (q + 1) % 2)
                    silu(i, q % 2)
                    if not (isinstance(i, int) and i == 0):
                        copy_hidT(i - 1, (q - 1) % 2)
                        copy_out(i - 1, (q - 1) % 4, k if q else k - 1)

                copy_slotT(0, 0)
                for q in range(4):
                    tile(q, q, 0)
                with act.Fori(1, TILES // 4 - 1) as k:
                    for q in range(4):
                        tile(k * 4 + q, q, k)
                for q in range(4):
                    tile(TILES - 4 + q, q, TILES // 4 - 1)
                copy_hidT(TILES - 1, 1)
                copy_out(TILES - 1, 3, TILES // 4 - 1)

                def stage_idx(g, b, k):
                    if isinstance(k, int) and k == 0:
                        act.wait_ge(s[f"scat{b}"], (m + 1) * NITER * 2 * G * DMA)
                    else:
                        act.wait_ge(s[f"gath{b}"], (m * NITER + k) * 2 * G * DMA)
                    A.activation(idx[:, b, :], SL[:, bass.ds(g * G, G), :].rearrange("p t k -> p (t k)"),
                                 ACT.Copy).then_inc(s["idx_done"], 1)

                for b in range(2):
                    stage_idx(b, b, 0)
                with act.Fori(1, NITER) as i:
                    for b in range(2):
                        stage_idx(i * 2 + b, b, i)

            moe(0)
            act.wait_ge(s["comb_done"], NG)
            act.wait_ge(s["negA_done"], 1)

            def step(ins):
                ins.then_inc(s["act_pre"], 1)

            def normT(p):
                act.wait_ge(s["xt_pre"], p + 1)
                wait(act, s["pe_pre"], done(PE_PRE, "z1_1", p - 1))
                src = bank[7][:, :].rearrange("p (s t) -> p s t", s=S)
                A.activation(xnT[:, 0, :, :], src, ACT.Copy).then_inc(s["act_norm"], 1)
                A.activation(xnT[:, 1, :, ::-1], src, ACT.Copy).then_inc(s["act_norm"], 1)

            def conv_start(p, r):
                wait(act, s["dve_pre"], done(DVE_PRE, "delta0", p) if r else done(DVE_PRE, "delta1", p - 1))
                for c in range(C):
                    act.wait_ge(s["pe_pre"], done(PE_PRE, f"xi{c}_{r}", p))
                    step(A.activation(tmp[:, c * W:(c + 1) * W], bank[6 + c][:, :], ACT.Identity,
                                      bias=ch[:, r, c, CB:CB + 1], scale=ch[:, r, c, 3:4]))

            def silus(p, r):
                if not isinstance(p, int) or 2 * p + r >= 2:
                    act.wait_ge(s["dve_post"], done(DVE_POST, "gate", 2 * p + r - 2))
                for c in range(C):
                    act.wait_ge(s["pe_pre"], done(PE_PRE, f"z{c}_{r}", p))
                    step(A.activation(zs[r][:, c * W:(c + 1) * W], bank[6 + c][:, :], ACT.Silu))
                act.wait_ge(s["dve_pre"], done(DVE_PRE, f"tap3c1_{r}", p))
                step(A.activation(xc[r], tmp, ACT.Silu))
                A.preload_act_table_set("natural_log_exp_and_others")

            def split_hi(p, r):
                act.wait_ge(s["pe_pre"], done(PE_PRE, f"xdbl{r}", p))
                step(A.activation(BCs[r][:, :], bank[6][0:2 * BC, :], ACT.Copy))
                step(A.activation(dts[2 * BC:2 * BC + RK, :], bank[6][2 * BC:2 * BC + RK, :], ACT.Copy))

            def softplus_parts(p, r):
                for c, bk in ((0, bank[7]), (1, bank[6])):
                    act.wait_ge(s["pe_pre"], done(PE_PRE, f"dt{c}_{r}", p))
                    step(A.activation(delta[r][:, c * W:(c + 1) * W], bk[:, :], ACT.Relu,
                                      bias=ch[:, r, c, DTB:DTB + 1]))
                    step(A.activation(tmp[:, c * W:(c + 1) * W], bk[:, :], ACT.Abs,
                                      bias=ch[:, r, c, DTB:DTB + 1]))

            def log1pexp(p, r):
                act.wait_ge(s["act_pre"], done(ACT_PRE, f"abs1_{r}", p))
                step(A.activation(tmp, tmp, ACT.Exp, scale=-1.0))
                act.wait_ge(s["act_pre"], done(ACT_PRE, f"exp{r}", p))
                step(A.activation(tmp, tmp, ACT.Ln, bias=1.0))

            def decay(p, r, n):
                N = p * 2 * NS + r * NS + n
                wait(act, s["scan_done"], N + 1 - R)
                if n == 0:
                    act.wait_ge(s["dve_pre"], done(DVE_PRE, f"delta{r}", p))
                for c in range(C):
                    ins = A.activation(dA[:, n % R, c, :, 1:],
                                       delta[r][:, c * W:(c + 1) * W].rearrange("p (s t) -> p s t", s=S)[:, :, 1:],
                                       ACT.Exp, scale=negA[:, r, c, n:n + 1])
                ins.then_inc(s["dA_ready"], 1)

            def copy_C(p, r, n):
                N = p * 2 * NS + r * NS + n
                act.wait_ge(s["bcC_ready"], N + 1)
                wait(act, s["hC_ready"], N + 1 - R)
                A.activation(Cs[:, n % R, :], bank[2 + n % 2][:, :], ACT.Copy).then_inc(s["Cs_ready"], 1)

            def pair(p, first, last):
                for r in range(2):
                    pv, rv = (p, 1) if r == 0 else (p + 1, 0)
                    prep = not (last and r == 1)
                    for n in range(NS):
                        for f, lead in ((decay, DECAY_LEAD), (copy_C, COPY_LEAD)):
                            if n + lead < NS:
                                f(p, r, n + lead)
                            elif prep:
                                f(pv, rv, n + lead - NS)
                        if not prep:
                            continue
                        if n == ACT_AT["conv"]:
                            conv_start(pv, rv)
                        if n == ACT_AT["silus"]:
                            silus(pv, rv)
                        if n == ACT_AT["hi"]:
                            split_hi(pv, rv)
                        if n == ACT_AT["parts"]:
                            softplus_parts(pv, rv)
                        if n == ACT_AT["ln"]:
                            log1pexp(pv, rv)
                        if n == ACT_AT["xnT"] and r == 0 and not last:
                            normT(p + 1)

            normT(0)
            conv_start(0, 0)
            silus(0, 0)
            split_hi(0, 0)
            softplus_parts(0, 0)
            log1pexp(0, 0)
            for n in range(DECAY_LEAD):
                decay(0, 0, n)
            for n in range(COPY_LEAD):
                copy_C(0, 0, n)
            pair(0, True, False)
            with act.Fori(1, NP - 1) as p:
                pair(p, False, False)
            pair(NP - 1, False, True)
            act.wait_ge(s["y_done"], 2 * NP * NS)
            act.wait_ge(s["dve_post"], done(DVE_POST, "res", 2 * NP - 1))
            moe(1)

        @block.tensor
        def _(pe):
            M = nc.tensor
            pe.wait_ge(s["loaded_w"], 14 * DMA)
            pe.wait_ge(s["consts"], 3)

            def moe(m):
                def turn(g, b):
                    pe.wait_ge(s["xn_done"], m * NG + g + 1)
                    wait(pe, s["xnT_done"], m * NG + g - 1)
                    for t in range(G):
                        ins = M.transpose(bank[b][:, t * P:(t + 1) * P], rowsN[:, b, t, :], id_sb[:, :])
                    ins.then_inc(s["xt_done"], 1)

                def logits(g, b):
                    pe.wait_ge(s["xnT_done"], m * NG + g + 1)
                    wait(pe, s["logits_act"], m * NG + g - 1)
                    for t in range(G):
                        ins = M.matmul(bank[4 + b][:, t * E:(t + 1) * E], xnTr[:, b, t * P:(t + 1) * P],
                                       gate_sb[:, :], start=True, stop=True)
                    ins.then_inc(s["logit_done"], 1)

                turn(0, 0)
                for b in range(2):
                    turn(b + 1, 1 - b)
                    logits(b, b)
                with pe.Fori(1, NITER - 1) as i:
                    for b in range(2):
                        turn(i * 2 + b + 1, 1 - b)
                        logits(i * 2 + b, b)
                turn(NG - 1, 1)
                logits(NG - 2, 0)
                logits(NG - 1, 1)

                pe.wait_ge(s["mask_done"], m + 1)
                flat = MK[:, :, :].rearrange("p e t -> p (e t)")
                M.matmul(bank[6][:, 0:E * NT], tri_sb[:, :], flat, start=True, stop=True).then_inc(s["route_pe"], 1)
                M.matmul(bank[7][:, 0:E * NT], ones_sb[:, :], flat, start=True, stop=True).then_inc(s["route_pe"], 1)
                pe.wait_ge(s["experts_done"], m + 1)
                pe.wait_ge(s["loaded_w"], (14 + 2 * m) * DMA)

                def turn_slots(i, q, k):
                    pe.wait_ge(s[f"xin{q}"], (m * (TILES // 4) + k + 1) * DMA)
                    wait(pe, s["slotT_act"], m * TILES + i)
                    M.transpose(bank[4][:, 0:P], xin[:, q, :], id_sb[:, :]).then_inc(s["slotT_pe"], 1)

                def gate(i, b, e):
                    pe.wait_ge(s["slotT_act"], m * TILES + i + 1)
                    wait(pe, s["silu_act"], m * TILES + i - 1)
                    M.matmul(bank[b][:, :], xT[:, b, :], wg_sb[:, bass.ds(e * I, I)],
                             start=True, stop=True).then_inc(s["gate_pe"], 1)

                def up(i, b, e):
                    wait(pe, s["hid_dve"], m * TILES + i - 1)
                    M.matmul(bank[2 + b][:, :], xT[:, b, :], wu_sb[:, bass.ds(e * I, I)],
                             start=True, stop=True).then_inc(s["up_pe"], 1)

                def turn_hidden(i, b):
                    pe.wait_ge(s["hid_dve"], m * TILES + i + 1)
                    wait(pe, s["hidT_act"], m * TILES + i)
                    for c in range(IC):
                        ins = M.transpose(bank[5][:, c * P:(c + 1) * P], hid[:, b, c * P:(c + 1) * P], id_sb[:, :])
                    ins.then_inc(s["hidT_pe"], 1)

                def down(i, b, e):
                    pe.wait_ge(s["hidT_act"], m * TILES + i + 1)
                    wait(pe, s["yo_act"], m * TILES + i)
                    for c in range(IC):
                        ins = M.matmul(bank[6][:, 0:D], hT[:, b, c * P:(c + 1) * P],
                                       wd_sb[:, bass.ds(e * IC + c, 1), :].rearrange("p c d -> p (c d)"),
                                       start=(c == 0), stop=(c == IC - 1))
                    ins.then_inc(s["down_pe"], 1)

                def expert_of(i):
                    return pe.value_load(te[0:1, bass.ds(i, 1)], min_val=0, max_val=E - 1)

                def tile(i, q, k, e_last):
                    if not (isinstance(i, int) and i == TILES - 1):
                        turn_slots(i + 1, (q + 1) % 4, k + 1 if q == 3 else k)
                    e = expert_of(i)
                    gate(i, q % 2, e)
                    if not (isinstance(i, int) and i == 0):
                        turn_hidden(i - 1, (q - 1) % 2)
                    up(i, q % 2, e)
                    if not (isinstance(i, int) and i == 0):
                        down(i - 1, (q - 1) % 2, e_last)
                    return e

                turn_slots(0, 0, 0)
                e = None
                for q in range(4):
                    e = tile(q, q, 0, e)
                with pe.Fori(1, TILES // 4 - 1) as k:
                    e = expert_of(k * 4 - 1)
                    for q in range(4):
                        e = tile(k * 4 + q, q, k, e)
                e = expert_of(TILES - 5)
                for q in range(4):
                    e = tile(TILES - 4 + q, q, TILES // 4 - 1, e)
                turn_hidden(TILES - 1, 1)
                down(TILES - 1, 1, e)

            moe(0)
            pe.wait_ge(s["yo_act"], TILES)

            def turn_norm(p):
                pe.wait_ge(s["dve_norm"], done(DVE_NORM, "xn", p))
                if not (isinstance(p, int) and p == 0):
                    pe.wait_ge(s["act_pre"], done(ACT_PRE, "abs0_1", p - 1))
                for t in range(G):
                    ins = M.transpose(bank[7][:, t * P:(t + 1) * P], xn4[:, t, :], id_sb[:, :])
                ins.then_inc(s["xt_pre"], 1)

            def project_in(p, r, part):
                if part == 0:
                    pe.wait_ge(s["act_norm"], done(ACT_NORM, "xnTrev", p))
                    if r == 1:
                        pe.wait_ge(s["act_pre"], done(ACT_PRE, "abs1_0", p))
                    if not isinstance(p, int) or 2 * p + r >= 3:
                        pe.wait_ge(s["dve_post"], done(DVE_POST, "res", 2 * p + r - 3))
                else:
                    pe.wait_ge(s["dve_pre"], done(DVE_PRE, f"tap3c1_{r}", p))
                for c in range(C):
                    at = part * DI + c * P
                    M.matmul(bank[6 + c][:, :], in_sb[:, r, at:at + P],
                             xnT[:, r, :, :].rearrange("p s t -> p (s t)"),
                             start=True, stop=True).then_inc(s["pe_pre"], 1)

            def project_x(p, r):
                pe.wait_ge(s["act_pre"], done(ACT_PRE, f"xc{r}", p))
                for c in range(C):
                    ins = M.matmul(bank[6][0:2 * BC + RK, :], xp_sb[:, r, c, :], xc[r][:, c * W:(c + 1) * W],
                                   start=(c == 0), stop=(c == C - 1))
                ins.then_inc(s["pe_pre"], 1)

            def project_dt(p, r):
                pe.wait_ge(s["act_pre"], done(ACT_PRE, f"dts{r}", p))
                pe.wait_ge(s["dve_pre"], done(DVE_PRE, f"lo{r}", p))
                for c, bk in ((0, bank[7]), (1, bank[6])):
                    M.matmul(bk[:, :], dtp_sb[2 * BC:2 * BC + RK, r, c * P:(c + 1) * P],
                             dts[2 * BC:2 * BC + RK, :], start=True, stop=True).then_inc(s["pe_pre"], 1)

            def project_out(u, r, after):
                pe.wait_ge(s["dve_post"], done(DVE_POST, "gate", u))
                after()
                for t in range(G):
                    for c in range(C):
                        ins = M.matmul(bank[6][:, t * D:(t + 1) * D], gat[:, c * W + t * P:c * W + (t + 1) * P],
                                       out_sb[:, r, c, :], start=(c == 0), stop=(c == C - 1))
                ins.then_inc(s["pe_post"], 1)

            def spread(p, r, n):
                N = p * 2 * NS + r * NS + n
                if n == 0:
                    pe.wait_ge(s["dve_pre"], done(DVE_PRE, f"lo{r}", p))
                wait(pe, s["mul_done"], N - 1)
                M.matmul(bank[n % 2][:, :], sel[:, n:n + 1].broadcast_to([2 * BC, P]), BCs[r][:, :],
                         start=True, stop=True).then_inc(s["bcB_ready"], 1)
                wait(pe, s["Cs_ready"], N - 1)
                M.matmul(bank[2 + n % 2][:, :], sel[:, NS + n:NS + n + 1].broadcast_to([2 * BC, P]), BCs[r][:, :],
                         start=True, stop=True).then_inc(s["bcC_ready"], 1)

            def sum_states(p, r, n):
                N = p * 2 * NS + r * NS + n
                pe.wait_ge(s["hC_ready"], N + 1)
                if n == 0:
                    u = p * 2 + r
                    wait(pe, s["dve_post"], done(DVE_POST, "skip1", u - 1) if not isinstance(u, int) or u > 0 else 0)
                for c in range(C):
                    ins = M.matmul(bank[4 + c][:, :], id_sb[:, :], hC[:, n % R, c * W:(c + 1) * W],
                                   start=(n == 0), stop=(n == NS - 1), skip_group_check=True)
                ins.then_inc(s["y_done"], 1)

            def pair(p, first, last):
                for r in range(2):
                    u = p * 2 + r
                    pv, rv = (p, 1) if r == 0 else (p + 1, 0)
                    prep = not (last and r == 1)
                    for n in range(NS):
                        if n + SPREAD_LEAD < NS:
                            spread(p, r, n + SPREAD_LEAD)
                        elif prep:
                            spread(pv, rv, n + SPREAD_LEAD - NS)
                        if prep:
                            if n == PE_AT["xi"]:
                                project_in(pv, rv, 0)
                            if n == PE_AT["z"]:
                                project_in(pv, rv, 1)
                            if n == PE_AT["xdbl"]:
                                project_x(pv, rv)
                            if n == PE_AT["dt"]:
                                project_dt(pv, rv)
                        if n == PE_AT["out"] and not (first and r == 0):
                            project_out(u - 1, 1 - r, lambda: wait(
                                pe, s["act_pre"], done(ACT_PRE, f"abs1_{rv}", pv) if prep else 0))
                        if n == PE_AT["xt"] and r == 0 and not last:
                            turn_norm(p + 1)
                        if n >= SUM_LAG:
                            sum_states(p, r, n - SUM_LAG)
                        elif not (first and r == 0):
                            sum_states(p if r else p - 1, 1 - r, n - SUM_LAG + NS)

            turn_norm(0)
            project_in(0, 0, 0)
            project_in(0, 0, 1)
            project_x(0, 0)
            project_dt(0, 0)
            for n in range(SPREAD_LEAD):
                spread(0, 0, n)
            pair(0, True, False)
            with pe.Fori(1, NP - 1) as p:
                pair(p, False, False)
            pair(NP - 1, False, True)
            for n in range(NS - SUM_LAG, NS):
                sum_states(NP - 1, 1, n)
            project_out(2 * NP - 1, 1, lambda: pe.wait_ge(
                s["dve_post"], done(DVE_POST, "res", 2 * NP - 2)))
            pe.wait_ge(s["dve_post"], done(DVE_POST, "res", 2 * NP - 1))
            moe(1)


def kernel(**inputs):
    import numpy as np
    import concourse.bacc as bacc
    from concourse.bass_utils import run_bass_kernel_spmd

    a = {k.removeprefix("L0_"): np.asarray(v) for k, v in inputs.items()}
    x = a["attn_x"]
    T, D = x.shape[0] * x.shape[1], x.shape[2]
    wg, wu, wd = a["ffn_wg"], a["ffn_wu"], a["ffn_wd"]
    E, I, _ = wg.shape
    NT, IC = T // P, I // P
    NS, RK = a["attn_A_log1"].shape[1], a["attn_dtp_w1"].shape[1]
    DI = a["attn_A_log1"].shape[0]
    C = DI // P

    def chunks(v):
        return v.reshape(C, P, -1).transpose(1, 0, 2)

    def both(f):
        return np.ascontiguousarray(np.stack([f(1), f(2)]))

    def rows_bcbc_dt(w):
        return np.concatenate([w[RK:], w[RK:], w[:RK]], 0)

    tiles = -(-(-(-(2 * T + E * (P - 1)) // P)) // 4) * 4
    reset = np.ones((P, E, NT), np.float32)
    reset[:, :, 0] = 0.0
    arrays = {
        "x": x.reshape(T, D),
        "gateT": a["ffn_gate_w"].T,
        "wgT": wg.transpose(2, 0, 1).reshape(D, E * I),
        "wuT": wu.transpose(2, 0, 1).reshape(D, E * I),
        "wdT": wd.reshape(E, D, IC, P).transpose(3, 0, 2, 1).reshape(P, E * IC, D),
        "inT": both(lambda r: a[f"attn_in_w{r}"].T),
        "xpT": both(lambda r: chunks(rows_bcbc_dt(a[f"attn_xp_w{r}"]).T)),
        "dtpT": both(lambda r: a[f"attn_dtp_w{r}"].T),
        "chan": both(lambda r: chunks(np.concatenate(
            [a[f"attn_conv_w{r}"].reshape(DI, -1), a[f"attn_conv_b{r}"].reshape(DI, 1),
             a[f"attn_dtp_b{r}"].reshape(DI, 1), a[f"attn_Dvec{r}"].reshape(DI, 1),
             a[f"attn_A_log{r}"]], 1))),
        "outT": both(lambda r: chunks(a[f"attn_out_w{r}"].T)),
        "ident": np.eye(P, dtype=np.float32),
        "tri": np.triu(np.ones((P, P), np.float32), 1),
        "e_rank": np.tile(np.arange(E, 0, -1, dtype=np.float32), (P, 1)),
        "e_reset": reset.reshape(P, E * NT),
        "tile_rank": np.arange(tiles, dtype=np.float32).reshape(1, tiles),
    }
    nc = bacc.Bacc("TRN2", target_bir_lowering=False, num_devices=1)
    launch, args = {}, []
    for name, v in arrays.items():
        v = np.ascontiguousarray(v)
        launch[name] = v
        args.append(nc.dram_tensor(name, v.shape, mybir.dt.from_np(v.dtype), kind="ExternalInput").ap())
    out = nc.dram_tensor("out", (T, D), F32, kind="ExternalOutput").ap()
    macaron_kernel(nc, *args, out)
    r = run_bass_kernel_spmd(nc, [launch], core_ids=[0])
    return r.results[0]["out"].reshape(x.shape)
```

```python
from contextlib import ExitStack

import concourse.bass as bass
from concourse import mybir

F32 = mybir.dt.float32
F32R = mybir.dt.float32r
I32 = mybir.dt.int32
U32 = mybir.dt.uint32
ALU = mybir.AluOpType
ACT = mybir.ActivationFunctionType
AX_X = mybir.AxisListType.X
P = 128
DMA = 16
EPS = 1e-5

DVE_PRE = [f"{s}{r}" for r in (0, 1) for s in (
    "tap1c0_", "tap1c1_", "tap2c0_", "tap2c1_", "tap3c0_", "tap3c1_", "lo", "delta")]
ACT_PRE = [f"{s}{r}" for r in (0, 1) for s in (
    "conv0_", "conv1_", "zs0_", "zs1_", "xc", "hi", "relu0_", "abs0_", "relu1_", "abs1_",
    "exp", "ln")]
PE_PRE = [f"{s}{r}" for r in (0, 1) for s in (
    "xi0_", "xi1_", "z0_", "z1_", "xdbl", "dt0_", "dt1_")]
DVE_NORM = ["stats", "aggr", "vareps", "xn"]
ACT_NORM = ["xnT", "xnTrev"]
DVE_AT = {"taps": (1, 2, 3), "lo": 8, "size": 12, "res": 12, "stats": 7, "xn": 11}
POOL_AT = {"first": 3, "second": 5, "gate": 2, "rstd": 8, "du": 12}
ACT_AT = {"y": 1, "conv": 0, "silus": 6, "hi": 8, "parts": 10, "ln": 11, "xnT": 14}
PE_AT = {"xi": 0, "z": 5, "xdbl": 7, "dt": 9, "out": 11, "xt": 13}
DECAY_LEAD, COPY_LEAD, SPREAD_LEAD, SUM_LAG = 2, 1, 2, 2


def done(steps, name, turn):
    return turn * len(steps) + steps.index(name) + 1


def wait(eng, sem, value):
    if isinstance(value, int) and value <= 0:
        return
    eng.wait_ge(sem, value)


def macaron_kernel(nc, x, gateT, wgT, wuT, wdT, inT, xpT, dtpT, chan, outT, ident, tri, e_rank,
                   e_reset, tile_rank, dest, pad, out):
    T, D = x.shape
    L = 256
    NT = T // P
    NP = T // (2 * L)
    E = gateT.shape[1]
    I = wgT.shape[1] // E
    IC = I // P
    DI = inT.shape[2] // 2
    C = DI // P
    NS = 16
    RK = dtpT.shape[1]
    BC = 2 * NS
    LOW = 2 * BC
    ROWS = LOW + BC + RK
    S = 2
    W = S * L
    G = 4
    NG = NT // G
    HT = 2
    TP = HT * P
    TILES = -(-(2 * T + E * (TP - 1)) // TP)
    TILES = -(-TILES // 4) * 4
    assert D == P and C == 2 and I == 512 and W == 512 and NG == NP and NG % 2 == 0
    CONV, CB, DTB, DSK, ALOG = 0, 4, 5, 6, 7

    DX = D + 2
    xs = nc.dram_tensor("slot_rows", [TILES * TP, DX], F32, kind="Internal").ap()
    yt = nc.dram_tensor("token_outputs", [2 * T + 4 * TP, D], F32, kind="Internal").ap()

    with ExitStack() as ctx:
        def sb(name, shape, dt=F32):
            return ctx.enter_context(nc.sbuf_tensor(name, shape, dt))

        def sem(name):
            return ctx.enter_context(nc.semaphore(name))

        X = sb("X", [P, NT, D])
        wgu = sb("wgu", [P, 2 * E * I])
        wg_sb, wu_sb = wgu[:, 0:E * I], wgu[:, E * I:2 * E * I]
        wd_sb = sb("wd_sb", [P, E * IC, D])
        gate_sb = sb("gate_sb", [P, E])
        in_sb = sb("in_sb", [P, 2, 2 * DI])
        xp_sb = sb("xp_sb", [P, 2, C, ROWS])
        dtp_sb = sb("dtp_sb", [ROWS, 2, DI])
        dtp_parts = [sb(f"dtp_{k}", [ROWS, 2, DI], F32R) for k in ("high", "low")]
        out_sb = sb("out_sb", [P, 2, C, D])
        ch = sb("ch", [P, 2, C, ALOG + NS])
        negA = sb("negA", [P, 2, C, NS])
        skip_sb = sb("skip_sb", [P, 2, C, P])
        id_sb = sb("id_sb", [P, P])
        tri_sb = sb("tri_sb", [P, P])
        ones_sb = sb("ones_sb", [P, P])
        half = sb("half", [P, NT])
        dest_sb = sb("dest_sb", [P, NT, 2])
        pad_row = sb("pad_row", [P, DX])
        y_pair = sb("y_pair", [P, G, 2, D])
        ids = sb("ids", [P, 4, HT], U32)
        padding = sb("padding", [P, HT])
        slot_wt = sb("slot_wt", [P, 4, HT])
        sel = sb("sel", [ROWS, BC], F32R)
        assert 8 * C * W <= 2 * E * I
        unit = [wgu[:, k * C * W:(k + 1) * C * W] for k in range(8)]
        MV = sb("MV", [P, G, 2])
        st = sb("st", [P, G, 6])
        ve = sb("ve", [P, NT])
        rs = sb("rs", [P, NT])
        mean = sb("mean", [P, NT])
        best = sb("best", [P, 2, NT])
        wt = sb("wt", [P, 2, NT])
        rank_sb = sb("rank_sb", [P, E])
        er_sb = sb("er_sb", [P, E * NT])
        tn_sb = sb("tn_sb", [1, TILES])
        I1 = sb("I1", [P, 2, NT])
        cnt = sb("cnt", [P, 4, E])
        cnti = sb("cnti", [P, 2, E], I32)
        SLf = sb("SLf", [P, 2, NT])
        SL = sb("SL", [P, NT, 2], U32)
        tef = sb("tef", [1, TILES])
        te = sb("te", [1, TILES], I32)
        R = 4
        CW = C * W
        BUF = R * (3 * CW + W) + 3 * CW
        buf = sb("buf", [P, BUF])
        PARTS = 2 * TP + 2 * TP + 4 * I + 4 * I
        with nc.sbuf_tensor("parts", [P, PARTS], F32R) as parts:
            pass
        over = sb("over", [P, (R + 1) * CW])
        assert PARTS <= (R + 1) * CW

        def carve(at, n):
            return buf[:, at:at + n]

        xin = carve(0, 4 * HT * DX).rearrange("p (b h d) -> p b h d", h=HT, d=DX)
        x_hi = parts[:, 0:2 * TP].rearrange("p (b d) -> p b d", d=TP)
        x_lo = parts[:, 2 * TP:4 * TP].rearrange("p (b d) -> p b d", d=TP)
        w_hi = parts[:, 4 * TP:4 * TP + 4 * I].rearrange("p (b w) -> p b w", w=2 * I)
        w_lo = parts[:, 4 * TP + 4 * I:].rearrange("p (b w) -> p b w", w=2 * I)
        wd_e = carve(1040, 4 * IC * D).rearrange("p (b w) -> p b w", w=IC * D)
        sg = carve(3088, 2 * 2 * TP).rearrange("p (b w) -> p b w", w=2 * TP)
        hid = carve(4112, 2 * IC * TP).rearrange("p (b w) -> p b w", w=IC * TP)
        yo = carve(6160, 4 * HT * D).rearrange("p (b h d) -> p b h d", h=HT, d=D)
        rowsA = carve(7184, 4 * G * DX).rearrange("p (b k t d) -> p b k t d", k=2, t=G, d=DX)
        xnTr = carve(9264, 2 * G * P).rearrange("p (b d) -> p b d", d=G * P)
        rowsN = carve(10288, 2 * G * D).rearrange("p (b t d) -> p b t d", t=G, d=D)
        LG = carve(11312, NT * E).rearrange("p (t e) -> p t e", e=E)
        O12 = carve(11824, 2 * E * NT).rearrange("p (k e t) -> p k e t", k=2, e=E)
        MK = carve(12848, E * NT).rearrange("p (e t) -> p e t", e=E)
        CS = carve(13360, E * NT)
        ST = carve(13872, NT * 6).rearrange("p (t k) -> p t k", k=6)
        tc8 = buf[0:1, 14256:14256 + TILES * E].rearrange("p (t e) -> p t e", e=E)
        assert 14256 + TILES * E <= BUF
        y_in = carve(0, 8 * G * D).rearrange("p (b t k d) -> p b t k d", t=G, k=2, d=D)
        ZEROED = 4 * DMA
        idx = sb("idx", [P, 2, 2 * G], U32)

        dA = over[:, 0:R * CW].rearrange("p (b c s t) -> p b c s t", b=R, c=C, s=S)
        prod = carve(0, R * CW).rearrange("p (b w) -> p b w", b=R)
        hs = carve(R * CW, R * CW).rearrange("p (b w) -> p b w", b=R)
        hC = carve(2 * R * CW, R * CW).rearrange("p (b w) -> p b w", b=R)
        Cs = carve(3 * R * CW, R * W).rearrange("p (b w) -> p b w", b=R)
        rest = R * (3 * CW + W)
        tmp = over[:, R * CW:(R + 1) * CW]
        xnT = carve(rest, 2 * W).rearrange("p (b s t) -> p b s t", b=2, s=S)
        gat = carve(rest + CW, CW)
        xn4 = carve(rest + 2 * CW, W).rearrange("p (t d) -> p t d", d=D)
        BCs = [sb(f"BCs{r}", [ROWS, W], F32R) for r in (0, 1)]
        xc = [unit[0], unit[4]]
        zs = [unit[1], unit[5]]
        delta = [unit[2], unit[6]]
        du = [unit[3], unit[7]]

        bank = [ctx.enter_context(nc.psum_tensor(f"bank{i}", [P, 512], F32)) for i in range(8)]

        names = """
            scatter_turn out_turn aggr_turn loaded_x0 loaded_x1 loaded_x2 loaded_x3 loaded_s loaded_m
            loaded_w zeroed pad_in pad_done y_pair_in y_in0 y_in1 y_in2 y_in3 ids_done consts
            stats_done dve_norm act_norm xt_pre vareps_done rstd_done xn_done xt_done xnT_done
            logit_done logits_act route_dve route_pe route_act stage_done scat0 scat1 xin0 xin1 xin2
            xin3 st0 st1 st2 st3 turned_pe xhi_act xlo_dve whi_act wlo_dve pad_found gate_pe up_pe
            silu_act hid_dve down_pe yo_act comb_done comb_first stored diff_done mask_done slots_done
            experts_done expA_done pair_added dtp_zeroed skip_ready y_copied gated du_done dve_pre
            act_pre pe_pre rstd_pre res_done pe_post negA_done bcB_ready bcC_ready dA_ready mul_done
            scan_done Cs_ready hC_ready y_done""".split()
        s = {n: sem(n) for n in names}
        block = ctx.enter_context(nc.Block())

        NITER = NG // 2

        def clear_slots(eng):
            eng.wait_ge(s["pad_done"], 1)
            n = TILES * HT // 4
            for a in range(4):
                eng.dma_start(xs[a * n * P:(a + 1) * n * P, :].rearrange("(t p) d -> p t d", p=P),
                              pad_row[:, :].unsqueeze(1).broadcast_to([P, n, DX])).then_inc(s["zeroed"], DMA)

        @block.sync
        def _(sp):
            for dst, src in [(id_sb[:, :], ident), (tri_sb[:, :], tri), (gate_sb[:, :], gateT),
                             (rank_sb[:, :], e_rank), (er_sb[:, :], e_reset), (tn_sb[:, :], tile_rank),
                             (dest_sb[:, :, :], dest)]:
                sp.dma_start(dst, src).then_inc(s["loaded_s"], DMA)
            for j in range(4):
                t0, t1 = j * NT // 4, (j + 1) * NT // 4
                sp.dma_start(X[:, t0:t1, :], x[t0 * P:t1 * P, :].rearrange("(t p) d -> p t d", p=P)
                             ).then_inc(s[f"loaded_x{j}"], DMA)
            for dst, src in [(wg_sb, wgT), (wu_sb, wuT), (wd_sb[:, :, :], wdT)]:
                sp.dma_start(dst, src).then_inc(s["loaded_w"], DMA)
            sp.wait_ge(s["dtp_zeroed"], 1)
            for dst, src in [(in_sb[:, :, :], inT.rearrange("r p n -> p r n")),
                             (xp_sb[:, :, :, :], xpT.rearrange("r p c n -> p r c n")),
                             (dtp_sb[BC:BC + RK, :, :], dtpT.rearrange("r k n -> k r n")),
                             (dtp_sb[LOW + BC:, :, :], dtpT.rearrange("r k n -> k r n")),
                             (ch[:, :, :, :], chan.rearrange("r p c n -> p r c n")),
                             (out_sb[:, :, :, :], outT.rearrange("r p c n -> p r c n"))]:
                sp.dma_start(dst, src).then_inc(s["loaded_m"], DMA)

            def load_slots(m, i, b):
                wait(sp, s["turned_pe"], m * TILES + i - 3)
                wait(sp, s["ids_done"], m * TILES + i - 3)
                sp.dma_start(xin[:, b, :, :], xs[bass.ds(i * TP, TP), :].rearrange("(h p) d -> p h d", h=HT)
                             ).then_inc(s[f"xin{b}"], DMA)

            def experts(m):
                sp.wait_ge(s["scat0"], (m + 1) * NG // 2 * 2 * G * DMA)
                sp.wait_ge(s["scat1"], (m + 1) * NG // 2 * 2 * G * DMA)
                for i in range(4):
                    load_slots(m, i, i)
                with sp.Fori(1, TILES // 4) as k:
                    for b in range(4):
                        load_slots(m, k * 4 + b, b)

            def outputs_there(m):
                for b in range(4):
                    sp.wait_ge(s[f"st{b}"], (m + 1) * TILES // 4 * HT * DMA)

            def y_rows(g):
                return yt[bass.ds(g * (2 * G * P), 2 * G * P), :].rearrange("(t p k) d -> p t k d", p=P, k=2)

            experts(0)
            for b in range(4):
                sp.wait_ge(s[f"xin{b}"], TILES // 4 * DMA)
            clear_slots(sp)
            outputs_there(0)
            sp.dma_start(y_pair[:, :, :, :], y_rows(0)).then_inc(s["y_pair_in"], DMA)
            with sp.Fori(1, NP) as p:
                sp.wait_ge(s["pair_added"], 2 * p)
                sp.dma_start(y_pair[:, :, :, :], y_rows(p)).then_inc(s["y_pair_in"], DMA)
            sp.wait_ge(s["gated"], 2 * NP)
            sp.dma_start(wg_sb, wgT).then_inc(s["loaded_w"], DMA)
            sp.dma_start(wu_sb, wuT).then_inc(s["loaded_w"], DMA)
            experts(1)
            outputs_there(1)
            for g in range(NG + 3):
                if g < NG:
                    if g >= 4:
                        sp.wait_ge(s["comb_done"], g - 3)
                    sp.dma_start(y_in[:, g % 4, :, :, :], y_rows(g)).then_inc(s[f"y_in{g % 4}"], DMA)
                if g >= 3:
                    h = g - 3
                    sp.wait_ge(s["comb_done"], h + 1)
                    sp.dma_start(out[h * G * P:(h + 1) * G * P, :].rearrange("(t p) d -> p t d", p=P),
                                 X[:, h * G:(h + 1) * G, :]).then_inc(s["stored"], DMA)
            sp.wait_ge(s["stored"], NG * DMA)

        @block.gpsimd
        def _(pool):
            pool.memset(ones_sb[:, :], 1.0).then_inc(s["consts"], 1)
            pool.memset(half[:, :], -0.5).then_inc(s["consts"], 1)
            pool.memset(dtp_sb[:, :, :], 0.0).then_inc(s["dtp_zeroed"], 1)
            pool.memset(pad_row[:, 0:D], 0.0).then_inc(s["consts"], 1)
            pool.memset(pad_row[:, D + 1:DX], 0.0).then_inc(s["consts"], 1)
            pool.dma_start(pad_row[:, D:D + 1], pad).then_inc(s["pad_in"], DMA)
            pool.wait_ge(s["consts"], 4)
            pool.wait_ge(s["pad_in"], DMA)
            pool.sem_inc(s["pad_done"], 1)

            def moe(m):
                for j in range(4):
                    cols = slice(j * NT // 4, (j + 1) * NT // 4)
                    pool.wait_ge(s["vareps_done"], m * 4 + j + 1)
                    pool.tensor_tensor(rs[:, cols], ve[:, cols], half[:, cols], ALU.pow).then_inc(s["rstd_done"], 1)
                pool.wait_ge(s["zeroed"], (m + 1) * ZEROED)

                def scatter(g, b):
                    pool.wait_ge(s["stage_done"], m * NG + g + 1)
                    pool.sem_inc(s["scatter_turn"], 1)
                    for t in range(G):
                        for k in range(2):
                            pool.indirect_dma_start(
                                out=xs[:, :], out_offset=bass.IndirectOffsetOnAxis(
                                    ap=idx[:, b, 2 * t + k:2 * t + k + 1], axis=0),
                                in_=rowsA[:, b, k, t, :], in_offset=None).then_inc(s[f"scat{b}"], DMA)

                with pool.Fori(0, NITER) as i:
                    for b in range(2):
                        scatter(i * 2 + b, b)

                def put_outputs(k, q):
                    pool.wait_ge(s["yo_act"], m * TILES + k * 4 + q + 1)
                    pool.sem_inc(s["out_turn"], 1)
                    for h in range(HT):
                        pool.indirect_dma_start(
                            out=yt[:, :], out_offset=bass.IndirectOffsetOnAxis(ap=ids[:, q, h:h + 1], axis=0),
                            in_=yo[:, q, h, :], in_offset=None).then_inc(s[f"st{q}"], DMA)

                with pool.Fori(0, TILES // 4) as k:
                    for q in range(4):
                        put_outputs(k, q)

            moe(0)

            def rstd(p):
                pool.wait_ge(s["dve_norm"], done(DVE_NORM, "vareps", p))
                pool.tensor_tensor(rs[:, 0:G], ve[:, 0:G], half[:, 0:G], ALU.pow).then_inc(s["rstd_pre"], 1)

            def pair(p, first, last):
                for r in range(2):
                    for n in range(NS):
                        N = p * 2 * NS + r * NS + n
                        b = n % R
                        pool.wait_ge(s["scan_done"], N + 1)
                        pool.wait_ge(s["Cs_ready"], N + 1)
                        wait(pool, s["y_done"], N + 1 - R)
                        pool.tensor_tensor(hC[:, b, :].rearrange("p (c w) -> p c w", c=C),
                                           hs[:, b, :].rearrange("p (c w) -> p c w", c=C),
                                           Cs[:, b, :].unsqueeze(1).broadcast_to([P, C, W]),
                                           ALU.mult).then_inc(s["hC_ready"], 1)
                        if r == 0 and not last:
                            if n == POOL_AT["first"]:
                                combine(p + 1, 0)
                            if n == POOL_AT["second"]:
                                combine(p + 1, 1)
                        if n == POOL_AT["gate"] and not (first and r == 0):
                            gate(p * 2 + r - 1, 1 - r)
                        if n == POOL_AT["rstd"] and r == 0 and not last:
                            rstd(p + 1)
                        if n == POOL_AT["du"] and not (last and r == 1):
                            size_times_input(p + r, 1 - r)

            def combine(p, k):
                pool.wait_ge(s["y_pair_in"], (p + 1) * DMA)
                wait(pool, s["pair_added"], 2 * p + k)
                pool.sem_inc(s["out_turn"], 1)
                xt = X[:, bass.ds(p * G, G), :]
                pool.tensor_tensor(xt, xt, y_pair[:, :, k, :], ALU.add).then_inc(s["pair_added"], 1)

            def gate(u, r):
                pool.wait_ge(s["y_copied"], u + 1)
                pool.tensor_tensor(gat, gat, zs[r], ALU.mult).then_inc(s["gated"], 1)

            def size_times_input(p, r):
                pool.wait_ge(s["dve_pre"], done(DVE_PRE, f"delta{r}", p))
                pool.tensor_tensor(du[r], delta[r], xc[r], ALU.mult).then_inc(s["du_done"], 1)

            combine(0, 0)
            combine(0, 1)
            rstd(0)
            size_times_input(0, 0)
            pair(0, True, False)
            with pool.Fori(1, NP - 1) as p:
                pair(p, False, False)
            pair(NP - 1, False, True)
            gate(2 * NP - 1, 1)
            moe(1)

        @block.vector
        def _(dve):
            V = nc.vector
            seq = [0]

            def chain(ins, name="route_dve", count=0):
                if name == "route_dve":
                    seq[0] += 1
                    count = seq[0]
                ins.then_inc(s[name], 1)
                dve.wait_ge(s[name], count)

            dve.wait_ge(s["loaded_s"], 7 * DMA)
            dve.wait_ge(s["consts"], 2)
            V.tensor_copy(sel[0:LOW, :], id_sb[0:LOW, 0:BC])
            chain(V.tensor_copy(sel[LOW:ROWS, :], id_sb[LOW:ROWS, LOW:LOW + BC]))

            def moe(m):
                def stats(g):
                    for t in range(G):
                        ins = V.bn_stats(ST[:, bass.ds(g * G + t, 1), :], X[:, bass.ds(g * G + t, 1), :])
                    ins.then_inc(s["stats_done"], 1)

                def moments(j):
                    if m == 0:
                        dve.wait_ge(s[f"loaded_x{j}"], DMA)
                    with dve.Fori(j * NG // 4, (j + 1) * NG // 4) as g:
                        stats(g)
                    dve.wait_ge(s["stats_done"], m * NG + (j + 1) * NG // 4)
                    q = slice(j * NT // 4, (j + 1) * NT // 4)
                    chain(V.tensor_tensor(mean[:, q], ST[:, q, 1], ST[:, q, 4], ALU.add))
                    chain(V.tensor_tensor(ve[:, q], ST[:, q, 1], ST[:, q, 4], ALU.subtract))
                    chain(V.tensor_scalar(mean[:, q], mean[:, q], 0.5, None, ALU.mult))
                    chain(V.scalar_tensor_tensor(out=ve[:, q], in0=ve[:, q], scalar=0.25, in1=ve[:, q],
                                                 op0=ALU.mult, op1=ALU.mult))
                    chain(V.tensor_tensor(SLf[:, 0, q], ST[:, q, 2], ST[:, q, 5], ALU.add))
                    chain(V.scalar_tensor_tensor(out=ve[:, q], in0=SLf[:, 0, q], scalar=1.0 / D, in1=ve[:, q],
                                                 op0=ALU.mult, op1=ALU.add))
                    V.tensor_scalar(ve[:, q], ve[:, q], EPS, None, ALU.add).then_inc(s["vareps_done"], 1)

                def normalise(g, rows):
                    for t in range(G):
                        ins = V.tensor_scalar(rows[:, t:t + 1, :], X[:, bass.ds(g * G + t, 1), :],
                                              mean[:, bass.ds(g * G + t, 1)], rs[:, bass.ds(g * G + t, 1)],
                                              ALU.subtract, ALU.mult)
                    return ins

                def normalise_for_logits(g, b):
                    wait(dve, s["xt_done"], m * NG + g - 1)
                    normalise(g, rowsN[:, b, :, :]).then_inc(s["xn_done"], 1)

                moments(0)
                for j in range(4):
                    if j < 3:
                        moments(j + 1)
                    if m == 1 and j == 0:
                        post_residual(2 * NP - 1, NP - 1, 1)
                        dve.wait_ge(s["res_done"], 2 * NP)
                    dve.wait_ge(s["rstd_done"], m * 4 + j + 1)
                    lo, hi = j * NITER // 4, (j + 1) * NITER // 4
                    if j == 0:
                        for b in range(2):
                            normalise_for_logits(b, b)
                        lo = 1
                    if lo < hi:
                        with dve.Fori(lo, hi) as i:
                            for b in range(2):
                                normalise_for_logits(i * 2 + b, b)
                dve.wait_ge(s["logits_act"], (m + 1) * NG)

                LGe = LG[:, :, :].rearrange("p t e -> p e t")
                for k in range(2):
                    one = O12[:, k, :, :]
                    chain(V.tensor_reduce(best[:, k, :], LG[:, :, :], AX_X, ALU.max))
                    chain(V.tensor_tensor(one, LGe, best[:, k, :].unsqueeze(1).broadcast_to([P, E, NT]),
                                          ALU.is_equal))
                    chain(V.tensor_tensor(one, one, rank_sb[:, :].unsqueeze(2).broadcast_to([P, E, NT]), ALU.mult))
                    chain(V.tensor_reduce(I1[:, k, :], one.rearrange("p e t -> p t e"), AX_X, ALU.max))
                    chain(V.tensor_tensor(one, rank_sb[:, :].unsqueeze(2).broadcast_to([P, E, NT]),
                                          I1[:, k, :].unsqueeze(1).broadcast_to([P, E, NT]), ALU.is_equal))
                    if k == 0:
                        chain(V.scalar_tensor_tensor(out=LG[:, :, :], in0=one.rearrange("p e t -> p t e"),
                                                     scalar=-3e38, in1=LG[:, :, :], op0=ALU.mult, op1=ALU.add))
                chain(V.tensor_tensor(MK[:, :, :], O12[:, 0, :, :], O12[:, 1, :, :], ALU.add), "mask_done", m + 1)

                chain(V.tensor_tensor(SLf[:, 0, :], best[:, 1, :], best[:, 0, :], ALU.subtract), "diff_done", m + 1)
                dve.wait_ge(s["route_act"], m + 1)
                chain(V.tensor_scalar(SLf[:, 0, :], SLf[:, 1, :], 1.0, None, ALU.add))
                chain(V.reciprocal(SLf[:, 0, :], SLf[:, 0, :]))
                chain(V.tensor_scalar(wt[:, 0, :], SLf[:, 0, :], 0.5, None, ALU.mult))
                chain(V.tensor_tensor(wt[:, 1, :], wt[:, 0, :], SLf[:, 1, :], ALU.mult))
                dve.wait_ge(s["route_pe"], 2 * m + 2)
                tot = bank[7][:, 0:E * NT]
                chain(V.tensor_tensor_scan(CS[:, :], er_sb[:, :], tot, 0.0, ALU.mult, ALU.add))
                CS3 = CS[:, :].rearrange("p (e t) -> p e t", e=E)
                chain(V.tensor_scalar(cnti[:, 0, :], CS3[:, :, NT - 1], float(TP - 1), None, ALU.add))
                chain(V.tensor_scalar(cnti[:, 1, :], cnti[:, 0, :], TP.bit_length() - 1, None, ALU.logical_shift_right))
                chain(V.tensor_copy(cnt[:, 0, :], cnti[:, 1, :]))
                chain(V.tensor_tensor_scan(cnt[:, 1, :], ones_sb[:, 0:E], cnt[:, 0, :], 0.0, ALU.mult, ALU.add))
                chain(V.tensor_tensor(cnt[:, 2, :], cnt[:, 1, :], cnt[:, 0, :], ALU.subtract))
                chain(V.tensor_scalar(cnt[:, 3, :], cnt[:, 2, :], float(TP), None, ALU.mult))
                chain(V.tensor_tensor(CS[:, :], CS[:, :], tot, ALU.subtract))
                chain(V.tensor_tensor(CS[:, :], CS[:, :], bank[6][:, 0:E * NT], ALU.add))
                chain(V.tensor_tensor(CS3, CS3, cnt[:, 3, :].unsqueeze(2).broadcast_to([P, E, NT]), ALU.add))
                for k in range(2):
                    chain(V.tensor_tensor(O12[:, k, :, :], O12[:, k, :, :], CS3, ALU.mult))
                    chain(V.tensor_reduce(SLf[:, k, :], O12[:, k, :, :].rearrange("p e t -> p t e"), AX_X, ALU.add))
                chain(V.tensor_copy(SL[:, :, :], SLf[:, :, :].rearrange("p k t -> p t k")), "slots_done", m + 1)
                chain(V.tensor_tensor(tc8[:, :, :], tn_sb[:, :].unsqueeze(2).broadcast_to([1, TILES, E]),
                                      cnt[0:1, 1, :].unsqueeze(1).broadcast_to([1, TILES, E]), ALU.is_ge))
                chain(V.tensor_reduce(tef[:, :], tc8[:, :, :], AX_X, ALU.add))
                chain(V.tensor_scalar(te[:, :], tef[:, :], float(E - 1), None, ALU.min), "experts_done", m + 1)

                def stage(g, b, k):
                    wait(dve, s[f"scat{b}"], (m * NITER + k) * 2 * G * DMA)
                    for k in range(2):
                        normalise(g, rowsA[:, b, k, :, 0:D])
                    V.tensor_copy(rowsA[:, b, :, :, D], dest_sb[:, bass.ds(g * G, G), :].rearrange("p t k -> p k t"))
                    V.tensor_copy(rowsA[:, b, :, :, D + 1], wt[:, :, bass.ds(g * G, G)])
                    V.tensor_copy(idx[:, b, :], SL[:, bass.ds(g * G, G), :].rearrange("p t k -> p (t k)")
                                  ).then_inc(s["stage_done"], 1)

                for b in range(2):
                    stage(b, b, 0)
                with dve.Fori(1, NITER) as i:
                    for b in range(2):
                        stage(i * 2 + b, b, i)

                def slot_columns(i, q, k):
                    dve.wait_ge(s[f"xin{q}"], (m * (TILES // 4) + k + 1) * DMA)
                    wait(dve, s[f"st{q}"], (m * (TILES // 4) + k) * HT * DMA)
                    V.tensor_copy(slot_wt[:, q, :], xin[:, q, :, D + 1])
                    wait(dve, s["ids_done"], m * TILES + i)
                    for h in range(HT):
                        ins = V.tensor_scalar(padding[:, h:h + 1], xin[:, q, h, D:D + 1], float(2 * T),
                                              float((q * HT + h) * P), ALU.is_ge, ALU.mult)
                    ins.then_inc(s["pad_found"], 1)
                    dve.wait_ge(s["pad_found"], m * TILES + i + 1)
                    V.tensor_tensor(ids[:, q, :], xin[:, q, :, D], padding[:, :], ALU.add).then_inc(s["ids_done"], 1)

                def low_x(i, b):
                    dve.wait_ge(s["xhi_act"], m * TILES + i + 1)
                    wait(dve, s["up_pe"], 2 * (m * TILES + i) - 2)
                    V.tensor_tensor(x_lo[:, b, :], bank[6][:, 0:TP], x_hi[:, b, :].bitcast(F32),
                                    ALU.subtract).then_inc(s["xlo_dve"], 1)

                def expert_of(i):
                    return dve.value_load(te[0:1, bass.ds(i, 1)], min_val=0, max_val=E - 1)

                def low_w(i, q, e):
                    dve.wait_ge(s["whi_act"], m * TILES + i + 1)
                    wait(dve, s["up_pe"], 2 * (m * TILES + i) - 2)
                    for k, w in ((0, wg_sb), (1, wu_sb)):
                        V.tensor_tensor(w_lo[:, q % 2, k * I:(k + 1) * I], w[:, bass.ds(e * I, I)],
                                        w_hi[:, q % 2, k * I:(k + 1) * I].bitcast(F32), ALU.subtract)
                    wait(dve, s["down_pe"], m * TILES + i - 3)
                    V.tensor_copy(wd_e[:, q, :].rearrange("p (c d) -> p c d", d=D),
                                  wd_sb[:, bass.ds(e * IC, IC), :]).then_inc(s["wlo_dve"], 1)

                def hidden(i, b, h):
                    H = 2 * (m * TILES + i) + h
                    dve.wait_ge(s["silu_act"], H + 1)
                    dve.wait_ge(s["up_pe"], H + 1)
                    wait(dve, s["down_pe"], m * TILES + i - 1)
                    V.tensor_tensor(hid[:, b, h * 2 * TP:(h + 1) * 2 * TP], sg[:, h, :], bank[2 + h][:, :],
                                    ALU.mult).then_inc(s["hid_dve"], 1)

                def four(k):
                    for q in range(4):
                        i = k * 4 + q
                        more = not (isinstance(i, int) and i == TILES - 1)
                        if more:
                            e = expert_of(i + 1)
                            low_x(i + 1, (q + 1) % 2)
                        slot_columns(i, q, k)
                        if more:
                            low_w(i + 1, (q + 1) % 4, e)
                        hidden(i, q % 2, 0)
                        hidden(i, q % 2, 1)

                dve.wait_ge(s["loaded_w"], (3 + 2 * m) * DMA)
                low_x(0, 0)
                low_w(0, 0, expert_of(0))
                four(0)
                with dve.Fori(1, TILES // 4 - 1) as k:
                    four(k)
                four(TILES // 4 - 1)

            def combine(g, rows):
                xt = X[:, bass.ds(g * G, G), :]
                for k in range(2):
                    V.tensor_tensor(xt, xt, rows[:, :, k, :], ALU.add).then_inc(
                        s["comb_done" if k else "comb_first"], 1)
                    if k == 0:
                        dve.wait_ge(s["comb_first"], g + 1)

            moe(0)

            dve.wait_ge(s["loaded_m"], 6 * DMA)
            dve.wait_ge(s["expA_done"], 1)
            V.tensor_scalar(negA[:, :, :, :], negA[:, :, :, :], -1.0, None, ALU.mult).then_inc(s["negA_done"], 1)
            chain(V.tensor_copy(dtp_parts[0][:, :, :], dtp_sb[:, :, :]))
            V.tensor_tensor(dtp_parts[1][:, :, :], dtp_sb[:, :, :], dtp_parts[0][:, :, :].bitcast(F32), ALU.subtract)
            for r in range(2):
                for c in range(C):
                    ins = V.tensor_scalar(skip_sb[:, r, c, :], id_sb[:, :], ch[:, r, c, DSK:DSK + 1], None, ALU.mult)
            ins.then_inc(s["skip_ready"], 1)
            for b in range(4):
                dve.wait_ge(s[f"st{b}"], TILES // 4 * HT * DMA)
            chain(V.memset(dA[:, :, :, :, 0:1], 0.0))

            def step_done(name, turn):
                dve.wait_ge(s["dve_pre"], done(DVE_PRE, name, turn))

            def layernorm(p):
                wait(dve, s["dve_norm"], done(DVE_NORM, "xn", p - 1))
                dve.wait_ge(s["pair_added"], 2 * p + 2)
                dve.sem_inc(s["aggr_turn"], 1)
                for t in range(G):
                    ins = V.bn_stats(st[:, t, :], X[:, bass.ds(p * G + t, 1), :])
                ins.then_inc(s["dve_norm"], 1)
                dve.wait_ge(s["dve_norm"], done(DVE_NORM, "stats", p))
                dve.sem_inc(s["aggr_turn"], 1)
                for t in range(G):
                    ins = V.bn_aggr(MV[:, t, :], st[:, t, :])
                ins.then_inc(s["dve_norm"], 1)
                dve.wait_ge(s["dve_norm"], done(DVE_NORM, "aggr", p))
                V.tensor_scalar(ve[:, 0:G], MV[:, :, 1], EPS, None, ALU.add).then_inc(s["dve_norm"], 1)

            def normalise(p):
                dve.wait_ge(s["rstd_pre"], p + 1)
                wait(dve, s["xt_pre"], p)
                for t in range(G):
                    ins = V.tensor_scalar(xn4[:, t, :], X[:, bass.ds(p * G + t, 1), :], MV[:, t, 0:1],
                                          rs[:, t:t + 1], ALU.subtract, ALU.mult)
                ins.then_inc(s["dve_norm"], 1)

            def taps(p, r, j):
                for c in range(C):
                    acc = tmp.rearrange("p (c s t) -> p c s t", c=C, s=S)[:, c, :, j:]
                    xi = bank[6 + c][:, :].rearrange("p (s t) -> p s t", s=S)[:, :, 0:L - j]
                    if j == 1:
                        dve.wait_ge(s["act_pre"], done(ACT_PRE, f"conv1_{r}", p))
                    else:
                        step_done(f"tap{j - 1}c{c}_{r}", p)
                    V.scalar_tensor_tensor(out=acc, in0=xi, scalar=ch[:, r, c, 3 - j:4 - j], in1=acc,
                                           op0=ALU.mult, op1=ALU.add).then_inc(s["dve_pre"], 1)

            def split_lo(p, r):
                dve.wait_ge(s["act_pre"], done(ACT_PRE, f"hi{r}", p))
                V.tensor_tensor(BCs[r][LOW:ROWS, :], bank[6][LOW:ROWS, :], BCs[r][LOW:ROWS, :].bitcast(F32),
                                ALU.subtract).then_inc(s["dve_pre"], 1)

            def step_size(p, r):
                dve.wait_ge(s["act_pre"], done(ACT_PRE, f"ln{r}", p))
                V.tensor_tensor(delta[r], delta[r], tmp, ALU.add).then_inc(s["dve_pre"], 1)

            def post_residual(u, p, r):
                dve.wait_ge(s["pe_post"], u + 1)
                xp4 = X[:, bass.ds(p * G, G), :]
                V.tensor_tensor(xp4, xp4, bank[6][:, :].rearrange("p (t d) -> p t d", t=G),
                                ALU.add).then_inc(s["res_done"], 1)

            def product(p, r, n):
                N = p * 2 * NS + r * NS + n
                if n == 0:
                    dve.wait_ge(s["du_done"], p * 2 + r + 1)
                dve.wait_ge(s["bcB_ready"], N + 1)
                wait(dve, s["scan_done"], N + 1 - R)
                V.tensor_tensor(prod[:, n % R, :].rearrange("p (c w) -> p c w", c=C),
                                du[r].rearrange("p (c w) -> p c w", c=C),
                                bank[n % 2][:, :].unsqueeze(1).broadcast_to([P, C, W]),
                                ALU.mult).then_inc(s["mul_done"], 1)

            def scan(p, r, n):
                N = p * 2 * NS + r * NS + n
                b = n % R
                dve.wait_ge(s["dA_ready"], N + 1)
                wait(dve, s["hC_ready"], N + 1 - R)
                dve.wait_ge(s["mul_done"], N + 1)
                V.tensor_tensor_scan(hs[:, b, :], dA[:, b, :, :, :].rearrange("p c s t -> p (c s t)"),
                                     prod[:, b, :], 0.0, ALU.mult, ALU.add).then_inc(s["scan_done"], 1)

            def pair(p, first, last):
                for r in range(2):
                    u = p * 2 + r
                    pv, rv = (p, 1) if r == 0 else (p + 1, 0)
                    prep = not (last and r == 1)
                    for n in range(NS):
                        if n < NS - 1:
                            product(p, r, n + 1)
                        elif prep:
                            product(pv, rv, 0)
                        scan(p, r, n)
                        if not (first and r == 0):
                            if n == DVE_AT["res"]:
                                post_residual(u - 1, p - 1 if r == 0 else p, 1 - r)
                        if not prep:
                            continue
                        if n in DVE_AT["taps"]:
                            taps(pv, rv, n - DVE_AT["taps"][0] + 1)
                        if n == DVE_AT["lo"]:
                            split_lo(pv, rv)
                        if n == DVE_AT["size"]:
                            step_size(pv, rv)
                        if r == 0 and not last:
                            if n == DVE_AT["stats"]:
                                layernorm(p + 1)
                            if n == DVE_AT["xn"]:
                                normalise(p + 1)

            layernorm(0)
            normalise(0)
            for j in (1, 2, 3):
                taps(0, 0, j)
            split_lo(0, 0)
            step_size(0, 0)
            product(0, 0, 0)
            pair(0, True, False)
            with dve.Fori(1, NP - 1) as p:
                pair(p, False, False)
            pair(NP - 1, False, True)
            dve.wait_ge(s["hC_ready"], 2 * NP * NS)
            dve.wait_ge(s["res_done"], 2 * NP - 1)
            moe(1)

            def combine_group(g, b, k):
                dve.wait_ge(s[f"y_in{b}"], (k + 1) * DMA)
                combine(g, y_in[:, b, :, :, :])

            with dve.Fori(0, NG // 4) as k:
                for b in range(4):
                    combine_group(k * 4 + b, b, k)
            dve.wait_ge(s["comb_done"], NG)

        @block.scalar
        def _(act):
            A = nc.scalar

            def moe(m):
                def evacuate(g, b):
                    act.wait_ge(s["xt_done"], m * NG + g + 1)
                    wait(act, s["logit_done"], m * NG + g - 1)
                    A.activation(xnTr[:, b, :], bank[b][:, :], ACT.Copy).then_inc(s["xnT_done"], 1)

                def copy_logits(g, b):
                    act.wait_ge(s["logit_done"], m * NG + g + 1)
                    A.activation(LG[:, bass.ds(g * G, G), :], bank[4 + b][:, 0:G * E].rearrange("p (t e) -> p t e", e=E),
                                 ACT.Copy).then_inc(s["logits_act"], 1)

                evacuate(0, 0)
                if m == 0:
                    clear_slots(act)
                for b in range(2):
                    evacuate(b + 1, 1 - b)
                    copy_logits(b, b)
                with act.Fori(1, NITER - 1) as i:
                    for b in range(2):
                        evacuate(i * 2 + b + 1, 1 - b)
                        copy_logits(i * 2 + b, b)
                evacuate(NG - 1, 1)
                copy_logits(NG - 2, 0)
                copy_logits(NG - 1, 1)
                act.wait_ge(s["diff_done"], m + 1)
                A.activation(SLf[:, 1, :], SLf[:, 0, :], ACT.Exp).then_inc(s["route_act"], 1)
                act.wait_ge(s["experts_done"], m + 1)

                def high_x(i, b):
                    act.wait_ge(s["turned_pe"], m * TILES + i + 1)
                    wait(act, s["up_pe"], 2 * (m * TILES + i) - 2)
                    A.activation(x_hi[:, b, :], bank[6][:, 0:TP], ACT.Copy).then_inc(s["xhi_act"], 1)

                def expert_of(i):
                    return act.value_load(te[0:1, bass.ds(i, 1)], min_val=0, max_val=E - 1)

                def high_w(i, b, e):
                    wait(act, s["up_pe"], 2 * (m * TILES + i) - 2)
                    wait(act, s["wlo_dve"], m * TILES + i - 1)
                    for k, w in ((0, wg_sb), (1, wu_sb)):
                        ins = A.activation(w_hi[:, b, k * I:(k + 1) * I], w[:, bass.ds(e * I, I)], ACT.Copy)
                    ins.then_inc(s["whi_act"], 1)

                def silu(i, h):
                    H = 2 * (m * TILES + i) + h
                    act.wait_ge(s["gate_pe"], H + 1)
                    wait(act, s["hid_dve"], H - 1)
                    A.activation(sg[:, h, :], bank[h][:, :], ACT.Silu).then_inc(s["silu_act"], 1)

                def copy_out(i, q, k):
                    act.wait_ge(s["down_pe"], m * TILES + i + 1)
                    wait(act, s[f"st{q}"], (m * (TILES // 4) + k) * HT * DMA)
                    act.wait_ge(s["ids_done"], m * TILES + i + 1)
                    for h in range(HT):
                        ins = A.activation(yo[:, q, h, :], bank[7][:, h * D:(h + 1) * D], ACT.Copy,
                                           scale=slot_wt[:, q, h:h + 1])
                    ins.then_inc(s["yo_act"], 1)

                def four(k):
                    for q in range(4):
                        i = k * 4 + q
                        more = not (isinstance(i, int) and i == TILES - 1)
                        if more:
                            e = expert_of(i + 1)
                            high_x(i + 1, (q + 1) % 2)
                            high_w(i + 1, (q + 1) % 2, e)
                        silu(i, 0)
                        if not (isinstance(i, int) and i == 0):
                            copy_out(i - 1, (q - 1) % 4, k if q else k - 1)
                        silu(i, 1)

                act.wait_ge(s["loaded_w"], (3 + 2 * m) * DMA)
                high_x(0, 0)
                high_w(0, 0, expert_of(0))
                four(0)
                with act.Fori(1, TILES // 4 - 1) as k:
                    four(k)
                four(TILES // 4 - 1)
                copy_out(TILES - 1, 3, TILES // 4 - 1)

            moe(0)
            act.wait_ge(s["loaded_m"], 6 * DMA)
            A.activation(negA[:, :, :, :], ch[:, :, :, ALOG:ALOG + NS], ACT.Exp).then_inc(s["expA_done"], 1)
            act.wait_ge(s["negA_done"], 1)

            def step(ins):
                ins.then_inc(s["act_pre"], 1)

            def normT(p):
                act.wait_ge(s["xt_pre"], p + 1)
                wait(act, s["pe_pre"], done(PE_PRE, "z1_1", p - 1))
                src = bank[7][:, :].rearrange("p (s t) -> p s t", s=S)
                A.activation(xnT[:, 0, :, :], src, ACT.Copy).then_inc(s["act_norm"], 1)
                A.activation(xnT[:, 1, :, ::-1], src, ACT.Copy).then_inc(s["act_norm"], 1)

            def conv_start(p, r):
                wait(act, s["dve_pre"], done(DVE_PRE, "delta0", p) if r else done(DVE_PRE, "delta1", p - 1))
                for c in range(C):
                    act.wait_ge(s["pe_pre"], done(PE_PRE, f"xi{c}_{r}", p))
                    step(A.activation(tmp[:, c * W:(c + 1) * W], bank[6 + c][:, :], ACT.Identity,
                                      bias=ch[:, r, c, CB:CB + 1], scale=ch[:, r, c, 3:4]))

            def silus(p, r):
                if not isinstance(p, int) or 2 * p + r >= 2:
                    act.wait_ge(s["gated"], 2 * p + r - 1)
                for c in range(C):
                    act.wait_ge(s["pe_pre"], done(PE_PRE, f"z{c}_{r}", p))
                    step(A.activation(zs[r][:, c * W:(c + 1) * W], bank[6 + c][:, :], ACT.Silu))
                act.wait_ge(s["dve_pre"], done(DVE_PRE, f"tap3c1_{r}", p))
                step(A.activation(xc[r], tmp, ACT.Silu))
                A.preload_act_table_set("natural_log_exp_and_others")

            def split_hi(p, r):
                act.wait_ge(s["pe_pre"], done(PE_PRE, f"xdbl{r}", p))
                step(A.activation(BCs[r][:, :], bank[6][0:ROWS, :], ACT.Copy))

            def softplus_parts(p, r):
                for c, bk in ((0, bank[7]), (1, bank[6])):
                    act.wait_ge(s["pe_pre"], done(PE_PRE, f"dt{c}_{r}", p))
                    step(A.activation(delta[r][:, c * W:(c + 1) * W], bk[:, :], ACT.Relu,
                                      bias=ch[:, r, c, DTB:DTB + 1]))
                    step(A.activation(tmp[:, c * W:(c + 1) * W], bk[:, :], ACT.Abs,
                                      bias=ch[:, r, c, DTB:DTB + 1]))

            def log1pexp(p, r):
                act.wait_ge(s["act_pre"], done(ACT_PRE, f"abs1_{r}", p))
                step(A.activation(tmp, tmp, ACT.Exp, scale=-1.0))
                act.wait_ge(s["act_pre"], done(ACT_PRE, f"exp{r}", p))
                step(A.activation(tmp, tmp, ACT.Ln, bias=1.0))

            def decay(p, r, n):
                N = p * 2 * NS + r * NS + n
                wait(act, s["scan_done"], N + 1 - R)
                if n == 0:
                    act.wait_ge(s["dve_pre"], done(DVE_PRE, f"delta{r}", p))
                for c in range(C):
                    ins = A.activation(dA[:, n % R, c, :, 1:],
                                       delta[r][:, c * W:(c + 1) * W].rearrange("p (s t) -> p s t", s=S)[:, :, 1:],
                                       ACT.Exp, scale=negA[:, r, c, n:n + 1])
                ins.then_inc(s["dA_ready"], 1)

            def copy_C(p, r, n):
                N = p * 2 * NS + r * NS + n
                act.wait_ge(s["bcC_ready"], N + 1)
                wait(act, s["hC_ready"], N + 1 - R)
                A.activation(Cs[:, n % R, :], bank[2 + n % 2][:, :], ACT.Copy).then_inc(s["Cs_ready"], 1)

            def copy_y(u):
                act.wait_ge(s["y_done"], (u + 1) * NS)
                wait(act, s["pe_post"], u)
                for c in range(C):
                    ins = A.activation(gat[:, c * W:(c + 1) * W], bank[4 + c][:, :], ACT.Copy)
                ins.then_inc(s["y_copied"], 1)

            def pair(p, first, last):
                for r in range(2):
                    pv, rv = (p, 1) if r == 0 else (p + 1, 0)
                    prep = not (last and r == 1)
                    for n in range(NS):
                        for f, lead in ((decay, DECAY_LEAD), (copy_C, COPY_LEAD)):
                            if n + lead < NS:
                                f(p, r, n + lead)
                            elif prep:
                                f(pv, rv, n + lead - NS)
                        if n == ACT_AT["y"] and not (first and r == 0):
                            copy_y(p * 2 + r - 1)
                        if not prep:
                            continue
                        if n == ACT_AT["conv"]:
                            conv_start(pv, rv)
                        if n == ACT_AT["silus"]:
                            silus(pv, rv)
                        if n == ACT_AT["hi"]:
                            split_hi(pv, rv)
                        if n == ACT_AT["parts"]:
                            softplus_parts(pv, rv)
                        if n == ACT_AT["ln"]:
                            log1pexp(pv, rv)
                        if n == ACT_AT["xnT"] and r == 0 and not last:
                            normT(p + 1)

            normT(0)
            conv_start(0, 0)
            silus(0, 0)
            split_hi(0, 0)
            softplus_parts(0, 0)
            log1pexp(0, 0)
            for n in range(DECAY_LEAD):
                decay(0, 0, n)
            for n in range(COPY_LEAD):
                copy_C(0, 0, n)
            pair(0, True, False)
            with act.Fori(1, NP - 1) as p:
                pair(p, False, False)
            pair(NP - 1, False, True)
            copy_y(2 * NP - 1)
            act.wait_ge(s["res_done"], 2 * NP)
            moe(1)

        @block.tensor
        def _(pe):
            M = nc.tensor
            pe.wait_ge(s["loaded_s"], 7 * DMA)
            pe.wait_ge(s["consts"], 2)

            def moe(m):
                def turn(g, b):
                    pe.wait_ge(s["xn_done"], m * NG + g + 1)
                    wait(pe, s["xnT_done"], m * NG + g - 1)
                    for t in range(G):
                        ins = M.transpose(bank[b][:, t * P:(t + 1) * P], rowsN[:, b, t, :], id_sb[:, :])
                    ins.then_inc(s["xt_done"], 1)

                def logits(g, b):
                    pe.wait_ge(s["xnT_done"], m * NG + g + 1)
                    wait(pe, s["logits_act"], m * NG + g - 1)
                    for t in range(G):
                        ins = M.matmul(bank[4 + b][:, t * E:(t + 1) * E], xnTr[:, b, t * P:(t + 1) * P],
                                       gate_sb[:, :], start=True, stop=True)
                    ins.then_inc(s["logit_done"], 1)

                turn(0, 0)
                for b in range(2):
                    turn(b + 1, 1 - b)
                    logits(b, b)
                with pe.Fori(1, NITER - 1) as i:
                    for b in range(2):
                        turn(i * 2 + b + 1, 1 - b)
                        logits(i * 2 + b, b)
                turn(NG - 1, 1)
                logits(NG - 2, 0)
                logits(NG - 1, 1)

                pe.wait_ge(s["mask_done"], m + 1)
                flat = MK[:, :, :].rearrange("p e t -> p (e t)")
                M.matmul(bank[6][:, 0:E * NT], tri_sb[:, :], flat, start=True, stop=True).then_inc(s["route_pe"], 1)
                M.matmul(bank[7][:, 0:E * NT], ones_sb[:, :], flat, start=True, stop=True).then_inc(s["route_pe"], 1)
                pe.wait_ge(s["experts_done"], m + 1)
                pe.wait_ge(s["loaded_w"], (3 + 2 * m) * DMA)

                def turn_slots(i, q, k):
                    pe.wait_ge(s[f"xin{q}"], (m * (TILES // 4) + k + 1) * DMA)
                    wait(pe, s["xlo_dve"], m * TILES + i)
                    for h in range(HT):
                        ins = M.transpose(bank[6][:, h * P:(h + 1) * P], xin[:, q, h, 0:D], id_sb[:, :])
                    ins.then_inc(s["turned_pe"], 1)

                def product(bk, b, at):
                    for c in range(2):
                        cols = slice(at + c * P, at + (c + 1) * P)
                        for j, (w, xx) in enumerate(((w_hi, x_hi), (w_hi, x_lo), (w_lo, x_hi))):
                            ins = M.matmul(bk[:, c * TP:(c + 1) * TP], w[:, b, cols],
                                           xx[:, b, :], start=(j == 0), stop=(j == 2))
                    return ins

                def gate(i, b, h):
                    H = 2 * (m * TILES + i) + h
                    if h == 0:
                        pe.wait_ge(s["xlo_dve"], m * TILES + i + 1)
                        pe.wait_ge(s["wlo_dve"], m * TILES + i + 1)
                    wait(pe, s["silu_act"], H - 1)
                    product(bank[h], b, h * 2 * P).then_inc(s["gate_pe"], 1)

                def up(i, b, h):
                    wait(pe, s["hid_dve"], 2 * (m * TILES + i) + h - 1)
                    product(bank[2 + h], b, I + h * 2 * P).then_inc(s["up_pe"], 1)

                def down(i, b, q):
                    pe.wait_ge(s["hid_dve"], 2 * (m * TILES + i) + 2)
                    wait(pe, s["yo_act"], m * TILES + i)
                    for h in range(HT):
                        for c in range(IC):
                            ins = M.matmul(bank[7][:, h * D:(h + 1) * D],
                                           hid[:, b, c * TP + h * P:c * TP + (h + 1) * P],
                                           wd_e[:, q, c * D:(c + 1) * D], start=(c == 0), stop=(c == IC - 1))
                    ins.then_inc(s["down_pe"], 1)

                def four(k):
                    for q in range(4):
                        i = k * 4 + q
                        if not (isinstance(i, int) and i == TILES - 1):
                            turn_slots(i + 1, (q + 1) % 4, k + 1 if q == 3 else k)
                        gate(i, q % 2, 0)
                        up(i, q % 2, 0)
                        if not (isinstance(i, int) and i == 0):
                            down(i - 1, (q - 1) % 2, (q - 1) % 4)
                        gate(i, q % 2, 1)
                        up(i, q % 2, 1)

                turn_slots(0, 0, 0)
                four(0)
                with pe.Fori(1, TILES // 4 - 1) as k:
                    four(k)
                four(TILES // 4 - 1)
                down(TILES - 1, 1, 3)

            moe(0)
            pe.wait_ge(s["yo_act"], TILES)
            pe.wait_ge(s["loaded_m"], 6 * DMA)

            def turn_norm(p):
                pe.wait_ge(s["dve_norm"], done(DVE_NORM, "xn", p))
                if not (isinstance(p, int) and p == 0):
                    pe.wait_ge(s["act_pre"], done(ACT_PRE, "abs0_1", p - 1))
                for t in range(G):
                    ins = M.transpose(bank[7][:, t * P:(t + 1) * P], xn4[:, t, :], id_sb[:, :])
                ins.then_inc(s["xt_pre"], 1)

            def project_in(p, r, part):
                if part == 0:
                    pe.wait_ge(s["act_norm"], done(ACT_NORM, "xnTrev", p))
                    if r == 1:
                        pe.wait_ge(s["act_pre"], done(ACT_PRE, "abs1_0", p))
                    if not isinstance(p, int) or 2 * p + r >= 3:
                        pe.wait_ge(s["res_done"], 2 * p + r - 2)
                else:
                    pe.wait_ge(s["dve_pre"], done(DVE_PRE, f"tap3c1_{r}", p))
                for c in range(C):
                    at = part * DI + c * P
                    M.matmul(bank[6 + c][:, :], in_sb[:, r, at:at + P],
                             xnT[:, r, :, :].rearrange("p s t -> p (s t)"),
                             start=True, stop=True).then_inc(s["pe_pre"], 1)

            def project_x(p, r):
                pe.wait_ge(s["act_pre"], done(ACT_PRE, f"xc{r}", p))
                for c in range(C):
                    ins = M.matmul(bank[6][0:ROWS, :], xp_sb[:, r, c, :], xc[r][:, c * W:(c + 1) * W],
                                   start=(c == 0), stop=(c == C - 1))
                ins.then_inc(s["pe_pre"], 1)

            def project_dt(p, r):
                pe.wait_ge(s["dve_pre"], done(DVE_PRE, f"lo{r}", p))
                for c, bk in ((0, bank[7]), (1, bank[6])):
                    for k in range(2):
                        ins = M.matmul(bk[:, :], dtp_parts[k][:, r, c * P:(c + 1) * P], BCs[r][:, :],
                                       start=(k == 0), stop=(k == 1))
                    ins.then_inc(s["pe_pre"], 1)

            def project_out(u, r, after):
                pe.wait_ge(s["gated"], u + 1)
                after()
                for t in range(G):
                    for c in range(C):
                        ins = M.matmul(bank[6][:, t * D:(t + 1) * D], gat[:, c * W + t * P:c * W + (t + 1) * P],
                                       out_sb[:, r, c, :], start=(c == 0), stop=(c == C - 1))
                ins.then_inc(s["pe_post"], 1)

            def spread(p, r, n):
                N = p * 2 * NS + r * NS + n
                if n == 0:
                    pe.wait_ge(s["dve_pre"], done(DVE_PRE, f"lo{r}", p))
                wait(pe, s["mul_done"], N - 1)
                M.matmul(bank[n % 2][:, :], sel[:, n:n + 1].broadcast_to([ROWS, P]), BCs[r][:, :],
                         start=True, stop=True).then_inc(s["bcB_ready"], 1)
                wait(pe, s["Cs_ready"], N - 1)
                M.matmul(bank[2 + n % 2][:, :], sel[:, NS + n:NS + n + 1].broadcast_to([ROWS, P]), BCs[r][:, :],
                         start=True, stop=True).then_inc(s["bcC_ready"], 1)

            def sum_states(p, r, n):
                N = p * 2 * NS + r * NS + n
                if n == 0:
                    wait(pe, s["y_copied"], p * 2 + r)
                    for c in range(C):
                        M.matmul(bank[4 + c][:, :], skip_sb[:, r, c, :], xc[r][:, c * W:(c + 1) * W],
                                 start=True, stop=False, skip_group_check=True)
                pe.wait_ge(s["hC_ready"], N + 1)
                for c in range(C):
                    ins = M.matmul(bank[4 + c][:, :], id_sb[:, :], hC[:, n % R, c * W:(c + 1) * W],
                                   start=False, stop=(n == NS - 1), skip_group_check=True)
                ins.then_inc(s["y_done"], 1)

            def pair(p, first, last):
                for r in range(2):
                    u = p * 2 + r
                    pv, rv = (p, 1) if r == 0 else (p + 1, 0)
                    prep = not (last and r == 1)
                    for n in range(NS):
                        if n + SPREAD_LEAD < NS:
                            spread(p, r, n + SPREAD_LEAD)
                        elif prep:
                            spread(pv, rv, n + SPREAD_LEAD - NS)
                        if prep:
                            if n == PE_AT["xi"]:
                                project_in(pv, rv, 0)
                            if n == PE_AT["z"]:
                                project_in(pv, rv, 1)
                            if n == PE_AT["xdbl"]:
                                project_x(pv, rv)
                            if n == PE_AT["dt"]:
                                project_dt(pv, rv)
                        if n == PE_AT["out"] and not (first and r == 0):
                            project_out(u - 1, 1 - r, lambda: wait(
                                pe, s["act_pre"], done(ACT_PRE, f"abs1_{rv}", pv) if prep else 0))
                        if n == PE_AT["xt"] and r == 0 and not last:
                            turn_norm(p + 1)
                        if n >= SUM_LAG:
                            sum_states(p, r, n - SUM_LAG)
                        elif not (first and r == 0):
                            sum_states(p if r else p - 1, 1 - r, n - SUM_LAG + NS)

            turn_norm(0)
            project_in(0, 0, 0)
            project_in(0, 0, 1)
            project_x(0, 0)
            project_dt(0, 0)
            for n in range(SPREAD_LEAD):
                spread(0, 0, n)
            pe.wait_ge(s["skip_ready"], 1)
            pair(0, True, False)
            with pe.Fori(1, NP - 1) as p:
                pair(p, False, False)
            pair(NP - 1, False, True)
            for n in range(NS - SUM_LAG, NS):
                sum_states(NP - 1, 1, n)
            project_out(2 * NP - 1, 1, lambda: pe.wait_ge(
                s["res_done"], 2 * NP - 1))
            pe.wait_ge(s["res_done"], 2 * NP)
            moe(1)


def kernel(**inputs):
    import numpy as np
    import concourse.bacc as bacc
    from concourse.bass_utils import run_bass_kernel_spmd

    a = {k.removeprefix("L0_"): np.asarray(v) for k, v in inputs.items()}
    x = a["attn_x"]
    T, D = x.shape[0] * x.shape[1], x.shape[2]
    wg, wu, wd = a["ffn_wg"], a["ffn_wu"], a["ffn_wd"]
    E, I, _ = wg.shape
    NT, IC = T // P, I // P
    NS, RK = a["attn_A_log1"].shape[1], a["attn_dtp_w1"].shape[1]
    DI = a["attn_A_log1"].shape[0]
    C = DI // P

    def chunks(v):
        return v.reshape(C, P, -1).transpose(1, 0, 2)

    def both(f):
        return np.ascontiguousarray(np.stack([f(1), f(2)]))

    def rows_twice(w):
        one = np.concatenate([w[RK:], w[:RK]], 0)
        gap = np.zeros((4 * NS - len(one), w.shape[1]), w.dtype)
        return np.concatenate([one, gap, one], 0)

    tiles = -(-(-(-(2 * T + E * (2 * P - 1)) // (2 * P))) // 4) * 4
    reset = np.ones((P, E, NT), np.float32)
    reset[:, :, 0] = 0.0
    arrays = {
        "x": x.reshape(T, D),
        "gateT": a["ffn_gate_w"].T,
        "wgT": wg.transpose(2, 0, 1).reshape(D, E * I),
        "wuT": wu.transpose(2, 0, 1).reshape(D, E * I),
        "wdT": wd.reshape(E, D, IC, P).transpose(3, 0, 2, 1).reshape(P, E * IC, D),
        "inT": both(lambda r: a[f"attn_in_w{r}"].T),
        "xpT": both(lambda r: chunks(rows_twice(a[f"attn_xp_w{r}"]).T)),
        "dtpT": both(lambda r: a[f"attn_dtp_w{r}"].T),
        "chan": both(lambda r: chunks(np.concatenate(
            [a[f"attn_conv_w{r}"].reshape(DI, -1), a[f"attn_conv_b{r}"].reshape(DI, 1),
             a[f"attn_dtp_b{r}"].reshape(DI, 1), a[f"attn_Dvec{r}"].reshape(DI, 1),
             a[f"attn_A_log{r}"]], 1))),
        "outT": both(lambda r: chunks(a[f"attn_out_w{r}"].T)),
        "ident": np.eye(P, dtype=np.float32),
        "tri": np.triu(np.ones((P, P), np.float32), 1),
        "e_rank": np.tile(np.arange(E, 0, -1, dtype=np.float32), (P, 1)),
        "e_reset": reset.reshape(P, E * NT),
        "tile_rank": np.arange(tiles, dtype=np.float32).reshape(1, tiles),
        "dest": np.ascontiguousarray(np.arange(2 * T, dtype=np.float32).reshape(NT, P, 2).transpose(1, 0, 2)),
        "pad": (2 * T + np.arange(P, dtype=np.float32)).reshape(P, 1),
    }
    nc = bacc.Bacc("TRN2", target_bir_lowering=False, num_devices=1)
    launch, args = {}, []
    for name, v in arrays.items():
        v = np.ascontiguousarray(v)
        launch[name] = v
        args.append(nc.dram_tensor(name, v.shape, mybir.dt.from_np(v.dtype), kind="ExternalInput").ap())
    out = nc.dram_tensor("out", (T, D), F32, kind="ExternalOutput").ap()
    macaron_kernel(nc, *args, out)
    r = run_bass_kernel_spmd(nc, [launch], core_ids=[0])
    return r.results[0]["out"].reshape(x.shape)
```
